# Optimizing a Trainium2 kernel written in Bass

```python
import numpy as np
import jax
import jax.numpy as jnp

def _softmax(x, axis=-1):
    return jax.nn.softmax(x, axis=axis)

def _gelu(x):
    return jax.nn.gelu(x, approximate=True)

def _silu(x):
    return jax.nn.silu(x)

def _sigmoid(x):
    return jax.nn.sigmoid(x)

def _layernorm(x, axis=-1, eps=1e-05):
    m = jnp.mean(x, axis=axis, keepdims=True)
    v = jnp.var(x, axis=axis, keepdims=True)
    return (x - m) / jnp.sqrt(v + eps)

def _scatter_add(tgt, idx, src, axis=0):
    return tgt.at[idx].add(src)

def _segment_sum(src, seg, n):
    return jax.ops.segment_sum(src, seg, n)
kernel_name = 'mk_decoder_preln_d1_seqx_r4_629cdf'

def setup_inputs(seed: int=0):
    np.random.seed(seed)
    _w = jnp.asarray

    def _rec_inputs():
        import jax
        import jax.numpy as jnp
        _rk = jax.random.key(seed)
        x = 7.22e-05 + 1 * jax.random.normal(jax.random.fold_in(_rk, 1), (1, 2048, 256), jnp.float32)
        _lenS = 2048 - jax.random.randint(jax.random.fold_in(_rk, 7), (1,), 0, max(1, 2048 // 4) + 1, jnp.int32)
        _lenS2 = 1601 - jax.random.randint(jax.random.fold_in(_rk, 8), (1,), 0, max(1, 1601 // 4) + 1, jnp.int32)
        _ctx_1024P = jax.random.normal(jax.random.fold_in(_rk, 11), (1, 16, 256), jnp.float32)
        _ctx_1024c = jax.random.dirichlet(jax.random.fold_in(_rk, 511), 0.3 * jnp.ones((16,), jnp.float32), (1, 1601))
        _ctx_1024t = jnp.einsum('bsk,bkd->bsd', _ctx_1024c, _ctx_1024P)
        _ctx_1024t = _ctx_1024t * jax.lax.rsqrt(jnp.mean(jnp.square(_ctx_1024t)) + 1e-12) * 0.953939
        ctx_1024 = 4.13588e-05 + 0.999923 * (_ctx_1024t + 0.3 * jax.random.normal(jax.random.fold_in(_rk, 611), (1, 1601, 256), jnp.float32))
        return (x, ctx_1024)
    x, ctx_1024 = _rec_inputs()

    def _L0_attn_setup():
        import jax, jax.numpy as jnp
        import numpy as np
        B, T, D_MODEL, N_HEADS = (2, 512, 256, 16)
        key = jax.random.key(seed)
        ks = jax.random.split(key, 5)
        w_scale = 0.02
        return {'x': jax.random.normal(ks[0], (B, T, D_MODEL), jnp.float32), 'Wq': jax.random.normal(ks[1], (D_MODEL, D_MODEL), jnp.float32) * w_scale, 'Wk': jax.random.normal(ks[2], (D_MODEL, D_MODEL), jnp.float32) * w_scale, 'Wv': jax.random.normal(ks[3], (D_MODEL, D_MODEL), jnp.float32) * w_scale, 'Wo': jax.random.normal(ks[4], (D_MODEL, D_MODEL), jnp.float32) * w_scale}
    _L0_attn_all = _L0_attn_setup()
    _L0_attn_in = {k: v for k, v in _L0_attn_all.items() if k in ('Wq', 'Wk', 'Wv', 'Wo')}
    del _L0_attn_all

    def _L0_xattn_setup():
        import jax, jax.numpy as jnp
        import numpy as np
        N_HEAD, MODEL_DIM, KEY_DIM, VALUE_DIM = (16, 256, 64, 64)
        B, S = (4, 512)
        EPS = 1e-05
        TEMP = float(np.sqrt(KEY_DIM))
        key = jax.random.key(seed)
        ks = jax.random.split(key, 12)
        d = {'query': jax.random.normal(ks[0], (B, S, MODEL_DIM), jnp.float32), 'key': jax.random.normal(ks[1], (B, S, MODEL_DIM), jnp.float32), 'value': jax.random.normal(ks[2], (B, S, MODEL_DIM), jnp.float32), 'Wq': jax.random.normal(ks[3], (MODEL_DIM, N_HEAD * KEY_DIM), jnp.float32) * np.sqrt(2.0 / (MODEL_DIM + KEY_DIM)), 'bq': jnp.zeros((N_HEAD * KEY_DIM,), jnp.float32), 'Wk': jax.random.normal(ks[4], (MODEL_DIM, N_HEAD * KEY_DIM), jnp.float32) * np.sqrt(2.0 / (MODEL_DIM + KEY_DIM)), 'bk': jnp.zeros((N_HEAD * KEY_DIM,), jnp.float32), 'Wv': jax.random.normal(ks[5], (MODEL_DIM, N_HEAD * VALUE_DIM), jnp.float32) * np.sqrt(2.0 / (MODEL_DIM + VALUE_DIM)), 'bv': jnp.zeros((N_HEAD * VALUE_DIM,), jnp.float32), 'Wo': jax.random.normal(ks[6], (N_HEAD * VALUE_DIM, MODEL_DIM), jnp.float32) * np.sqrt(2.0 / (N_HEAD * VALUE_DIM + MODEL_DIM)), 'bo': jnp.zeros((MODEL_DIM,), jnp.float32), 'ln_gamma': jnp.ones((MODEL_DIM,), jnp.float32), 'ln_beta': jnp.zeros((MODEL_DIM,), jnp.float32)}
        return d
    _L0_xattn_all = _L0_xattn_setup()
    _L0_xattn_in = {k: v for k, v in _L0_xattn_all.items() if k in ('Wq', 'bq', 'Wk', 'bk', 'Wv', 'bv', 'Wo', 'bo', 'ln_gamma', 'ln_beta')}
    del _L0_xattn_all

    def _L0_ffn_setup():
        import jax, jax.numpy as jnp
        import numpy as np
        FEATURES = 256
        D_IN = 256

        def fp8_gemm_optimized(x, input_scale, kernel, kernel_scale):
            s_in = input_scale[0]
            s_k = kernel_scale[0]
            x_q = (x.astype(jnp.float32) / s_in).astype(jnp.float8_e4m3fn)
            k_q = (kernel.astype(jnp.float32) / s_k).astype(jnp.float8_e4m3fn)
            y = jnp.dot(x_q.astype(jnp.float32), k_q.astype(jnp.float32), preferred_element_type=jnp.float32)
            return y * (s_in * s_k)
        key = jax.random.key(seed)
        kx, kk, kb = jax.random.split(key, 3)
        x = jax.random.normal(kx, (4, 2048, D_IN), dtype=jnp.float32)
        limit = np.sqrt(6.0 / (D_IN + FEATURES)).astype(np.float32)
        kernel = jax.random.uniform(kk, (D_IN, FEATURES), dtype=jnp.float32, minval=-limit, maxval=limit).astype(jnp.bfloat16)
        input_scale = jnp.ones((1,), dtype=jnp.float32)
        kernel_scale = jnp.ones((1,), dtype=jnp.float32)
        bias = jnp.zeros((FEATURES,), dtype=jnp.bfloat16)
        return {'x': x, 'kernel': kernel, 'input_scale': input_scale, 'kernel_scale': kernel_scale, 'bias': bias}
    _L0_ffn_all = _L0_ffn_setup()
    _L0_ffn_in = {k: v for k, v in _L0_ffn_all.items() if k in ('kernel', 'input_scale', 'kernel_scale', 'bias')}
    del _L0_ffn_all
    return {'x': x, 'ctx_1024': ctx_1024, 'L0_attn_Wq': _L0_attn_in['Wq'], 'L0_attn_Wk': _L0_attn_in['Wk'], 'L0_attn_Wv': _L0_attn_in['Wv'], 'L0_attn_Wo': _L0_attn_in['Wo'], 'L0_xattn_Wq': _L0_xattn_in['Wq'], 'L0_xattn_bq': _L0_xattn_in['bq'], 'L0_xattn_Wk': _L0_xattn_in['Wk'], 'L0_xattn_bk': _L0_xattn_in['bk'], 'L0_xattn_Wv': _L0_xattn_in['Wv'], 'L0_xattn_bv': _L0_xattn_in['bv'], 'L0_xattn_Wo': _L0_xattn_in['Wo'], 'L0_xattn_bo': _L0_xattn_in['bo'], 'L0_xattn_ln_gamma': _L0_xattn_in['ln_gamma'], 'L0_xattn_ln_beta': _L0_xattn_in['ln_beta'], 'L0_ffn_kernel': _L0_ffn_in['kernel'], 'L0_ffn_input_scale': _L0_ffn_in['input_scale'], 'L0_ffn_kernel_scale': _L0_ffn_in['kernel_scale'], 'L0_ffn_bias': _L0_ffn_in['bias']}

def reference(x, ctx_1024, L0_attn_Wq, L0_attn_Wk, L0_attn_Wv, L0_attn_Wo, L0_xattn_Wq, L0_xattn_bq, L0_xattn_Wk, L0_xattn_bk, L0_xattn_Wv, L0_xattn_bv, L0_xattn_Wo, L0_xattn_bo, L0_xattn_ln_gamma, L0_xattn_ln_beta, L0_ffn_kernel, L0_ffn_input_scale, L0_ffn_kernel_scale, L0_ffn_bias):
    import jax
    import jax.numpy as jnp

    def _L0_attn_ref(x, Wq, Wk, Wv, Wo):
        import jax, jax.numpy as jnp
        import numpy as np
        B, T, D_MODEL, N_HEADS = (2, 512, 256, 16)
        Bv, Tv, _ = x.shape
        H = N_HEADS
        D = D_MODEL // H
        q = (x @ Wq.T).reshape(Bv, Tv, H, D).transpose(0, 2, 1, 3)
        k = (x @ Wk.T).reshape(Bv, Tv, H, D).transpose(0, 2, 1, 3)
        v = (x @ Wv.T).reshape(Bv, Tv, H, D).transpose(0, 2, 1, 3)
        scale = jnp.sqrt(jnp.asarray(D, jnp.float32))
        scores = jnp.einsum('bhqd,bhkd->bhqk', q, k) / scale
        slopes = jnp.asarray([2.0 ** (-8.0 * h / H) for h in range(1, H + 1)], jnp.float32)
        pos = jnp.arange(Tv)
        dist = jnp.abs(pos[None, :] - pos[:, None]).astype(jnp.float32)
        bias = -dist[None, :, :] * slopes[:, None, None]
        causal_mask = jnp.triu(jnp.ones((Tv, Tv), dtype=bool), 1)
        bias = jnp.where(causal_mask[None, :, :], -jnp.inf, bias)
        scores = scores + bias[None]
        attn = jax.nn.softmax(scores, axis=-1)
        out = jnp.einsum('bhqk,bhkd->bhqd', attn, v)
        out = out.transpose(0, 2, 1, 3).reshape(Bv, Tv, D_MODEL)
        return out @ Wo.T

    def _L0_xattn_ref(query, key, value, Wq, bq, Wk, bk, Wv, bv, Wo, bo, ln_gamma, ln_beta):
        import jax, jax.numpy as jnp
        import numpy as np
        N_HEAD, MODEL_DIM, KEY_DIM, VALUE_DIM = (16, 256, 64, 64)
        B, S = (4, 512)
        EPS = 1e-05
        TEMP = float(np.sqrt(KEY_DIM))
        b, sq, _ = query.shape
        residual = query
        q = (query @ Wq + bq).reshape(b, sq, N_HEAD, KEY_DIM)
        k = (key @ Wk + bk).reshape(b, key.shape[1], N_HEAD, KEY_DIM)
        v = (value @ Wv + bv).reshape(b, value.shape[1], N_HEAD, VALUE_DIM)
        scores = jnp.einsum('bqhd,bkhd->bhqk', q, k) / TEMP
        attn = jax.nn.softmax(scores, axis=-1)
        out = jnp.einsum('bhqk,bkhd->bqhd', attn, v).reshape(b, sq, N_HEAD * VALUE_DIM)
        out = out @ Wo + bo + residual
        mu = jnp.mean(out, axis=-1, keepdims=True)
        var = jnp.var(out, axis=-1, keepdims=True)
        return (out - mu) * jax.lax.rsqrt(var + EPS) * ln_gamma + ln_beta

    def _L0_ffn_ref(x, kernel, input_scale, kernel_scale, bias):
        import jax, jax.numpy as jnp
        import numpy as np
        FEATURES = 256
        D_IN = 256

        def fp8_gemm_optimized(x, input_scale, kernel, kernel_scale):
            s_in = input_scale[0]
            s_k = kernel_scale[0]
            x_q = (x.astype(jnp.float32) / s_in).astype(jnp.float8_e4m3fn)
            k_q = (kernel.astype(jnp.float32) / s_k).astype(jnp.float8_e4m3fn)
            y = jnp.dot(x_q.astype(jnp.float32), k_q.astype(jnp.float32), preferred_element_type=jnp.float32)
            return y * (s_in * s_k)
        dtype = jnp.bfloat16
        x = x.astype(dtype)
        orig_shape = x.shape
        x2 = x.reshape(-1, x.shape[-1])
        y = fp8_gemm_optimized(x2, input_scale, kernel, kernel_scale)
        y = y.astype(dtype) + bias
        return y.reshape(orig_shape[:-1] + (FEATURES,))
    x = x + _L0_attn_ref(_layernorm(x, axis=-1), L0_attn_Wq, L0_attn_Wk, L0_attn_Wv, L0_attn_Wo)
    x = x + _L0_xattn_ref(_layernorm(x, axis=-1), ctx_1024, ctx_1024, L0_xattn_Wq, L0_xattn_bq, L0_xattn_Wk, L0_xattn_bk, L0_xattn_Wv, L0_xattn_bv, L0_xattn_Wo, L0_xattn_bo, L0_xattn_ln_gamma, L0_xattn_ln_beta)
    x = x + _L0_ffn_ref(_layernorm(x, axis=-1), L0_ffn_kernel, L0_ffn_input_scale, L0_ffn_kernel_scale, L0_ffn_bias)
    return x

_drawn_inputs = setup_inputs


def setup_inputs(seed=0):
    import zlib

    import numpy as np

    out = dict(_drawn_inputs(seed))
    spreads = {'L0_xattn_bq': (0.0, 0.295),
     'L0_xattn_bk': (0.0, 0.8),
     'L0_xattn_bv': (0.0, 0.1),
     'L0_xattn_bo': (0.0, 0.1),
     'L0_xattn_ln_gamma': (1.0, 0.2),
     'L0_xattn_ln_beta': (0.0, 0.1),
     'L0_ffn_bias': (0.0, 0.1)}
    factors = {'L0_attn_Wq': 8.0, 'L0_attn_Wk': 8.0}
    for name, (base, spread) in spreads.items():
        noise = np.random.default_rng([zlib.crc32(name.encode()), seed]).standard_normal(out[name].shape)
        drawn = base * np.exp(spread * noise) if base else spread * noise
        out[name] = jnp.asarray(drawn.astype(out[name].dtype))
    for name, factor in factors.items():
        out[name] = (out[name] * factor).astype(out[name].dtype)
    return out
```

```python
from contextlib import ExitStack

import numpy as np

import concourse.bass as bass
from concourse import mybir

F32, F32R = mybir.dt.float32, mybir.dt.float32r
BF16, F16 = mybir.dt.bfloat16, mybir.dt.float16
ALU, ACT, AX = mybir.AluOpType, mybir.ActivationFunctionType, mybir.AxisListType

P = 128
T, D, S = 2048, 256, 1601
NT = T // P
DC = D // P
H = 16
DH1, DH2 = D // H, 64
NS = -(-S // P)
SE = S + S % 2
BQ = 512
NB, TB = T // BQ, BQ // P
LN_EPS = 1e-5
MASKED = -1.0e30
WEIGHT_BITS = 12
FP8_MAX = 448.0
FP8_MIN_NORMAL = 2.0 ** -6
ROUND_TO_3_BITS = 1.5 * 2.0 ** 20


MINUS_POS, POS, ONES, ZEROS = 2 * H, 2 * H + 2, 2 * H + 4, 2 * H + 6
STACKED = 4 * DH1


def slopes():
    return np.asarray([2.0 ** (-8.0 * h / H) for h in range(1, H + 1)], np.float32) * np.float32(4)


def alibi_rows():
    pos = np.arange(T, dtype=np.float32)
    whole = slopes()
    hi = (whole.view(np.uint32) & np.uint32(0xFFFFF000)).view(np.float32)
    rows = np.zeros((2 * H + 8, T), np.float32)
    rows[0:2 * H:2] = hi[:, None]
    rows[1:2 * H:2] = (whole - hi)[:, None]
    rows[MINUS_POS:MINUS_POS + 2], rows[POS:POS + 2], rows[ONES:ONES + 2] = -pos, pos, 1.0
    return rows


class Signal:

    def __init__(self, sem):
        self.sem, self.count = sem, 0

    def next(self, by):
        self.count += by
        return (self, self.count)


class Queue:

    def __init__(self):
        self.items = []

    def do(self, op, *args, waits=(), signal=None, by=1, **kw):
        token = signal.next(by) if signal else None
        self.items.append((op, args, kw, [w for w in waits if w], token, by))
        return token

    def run(self, engine):
        seen = {}
        for op, args, kw, waits, token, by in self.items:
            for sig, count in waits:
                if seen.get(id(sig), 0) < count:
                    seen[id(sig)] = count
                    engine.wait_ge(sig.sem, count)
            if op is not None:
                ins = op(*args, **kw)
                if token:
                    ins.then_inc(token[0].sem, by)


class Ring:

    def __init__(self, bufs):
        self.bufs, self.free, self.at = bufs, [()] * len(bufs), -1

    def take(self):
        self.at = (self.at + 1) % len(self.bufs)
        return self.bufs[self.at], self.free[self.at]

    def read_by(self, *tokens, slot=None):
        self.free[self.at if slot is None else slot] = tokens


def decoder(nc, ins, out):
    ctx = ExitStack()
    with ctx:
        _decoder(nc, ctx, ins, out)


def _decoder(nc, ctx, A, out):
    V, SC, G, TE, SY = nc.vector, nc.scalar, nc.gpsimd, nc.tensor, nc.sync
    pe, act, dve, pool, sp = Queue(), Queue(), Queue(), Queue(), Queue()

    def sb(name, shape, dt, stack=ctx):
        return stack.enter_context(nc.sbuf_tensor(name, shape, dt))

    def sig(name):
        return Signal(ctx.enter_context(nc.semaphore(name)))

    const_ready = sig("const_ready")
    pe_rows = sig("pe_rows")
    pe_scores = sig("pe_scores")
    pe_values = sig("pe_values")
    act_done = sig("act_done")
    exp_hi = sig("exp_hi")
    exp_full = sig("exp_full")
    lo_dve = sig("lo_dve")
    lo_pool = sig("lo_pool")
    dve_max = sig("dve_max")
    dve_done = sig("dve_done")
    pool_done = sig("pool_done")
    x_in = [sig(f"x_in{b}") for b in range(NB)]
    ctx_in = sig("ctx_in")
    w_self_in = sig("w_self_in")
    alibi_in = sig("alibi_in")
    small_in = sig("small_in")
    w_cross_in = [sig(f"w_cross_in{i}") for i in range(2)]
    w_head_in = [sig(f"w_head_in{i}") for i in range(2)]
    stack_in = [sig(f"stack_in{i}") for i in range(3)]
    maxrow_in = [sig(f"maxrow_in{i}") for i in range(3)]
    stored = sig("stored")

    x = sb("x", [P, NT, D], F32)
    ident = sb("ident", [P, P], F32)
    ident_bf = sb("ident_bf", [P, P], BF16)
    mask_rows = sb("mask_rows", [P, P], BF16)
    mask_cols = sb("mask_cols", [P, P], BF16)
    stats = sb("stats", [P, NT, 6], F32)
    meanvar = sb("meanvar", [P, NT, 2], F32)
    rstd = sb("rstd", [P, NT], F32)
    minus_half = sb("minus_half", [P, NT], F32)
    maxima = sb("maxima", [P, 2, NT, 2], F32)
    shift = sb("shift", [P, 2, NT], F32)
    shift_hi = sb("shift_hi", [NT, 2, P], F32R)
    shift_lo = sb("shift_lo", [NT, 2, P], F32R)
    w_full = [sb(f"w_full{i}", [P, BQ], F32) for i in range(3)]
    w_hi = [sb(f"w_hi{i}", [P, BQ], F16) for i in range(4)]
    w_lo = [sb(f"w_lo{i}", [P, BQ], F16) for i in range(4)]
    OW = 3 * DH2 + 2
    o_sb = Ring([sb(f"o_sb{i}", [P, TB, OW], F32) for i in range(2)])
    recip = sb("recip", [P, 2, TB], F32)
    norm_t = sb("norm_t", [P, DC, T], F32)
    o_t = Ring([sb("o_t", [P, DC, BQ], F32)])

    wide = Ring([ctx.enter_context(nc.psum_tensor(f"wide{i}", [P, 2 * BQ], F32)) for i in range(2)])
    scores = Ring([ctx.enter_context(nc.psum_tensor(f"scores{i}", [P, BQ], F32)) for i in range(2)])
    sums = ctx.enter_context(nc.psum_tensor("sums", [P, 2, BQ], F32))
    sums_free = []

    pool.do(G.memset, ident[:, :], 0.0, signal=const_ready)
    pool.do(G.memset, ident_bf[:, :], 0.0, signal=const_ready)
    pool.do(G.memset, mask_rows[:, :], 0.0, signal=const_ready)
    pool.do(G.memset, minus_half[:, :], -0.5, signal=const_ready)
    pool.do(G.memset, maxima[:, :, :, :], 4 * MASKED, signal=const_ready)
    zeroed = pool.do(G.memset, mask_cols[:, :], 0.0, signal=const_ready)
    for m in (ident, ident_bf):
        pool.do(G.affine_select, out=m[:, :], in_=m[:, :], compare_op=ALU.not_equal, fill=1.0, base=0,
                pattern=[[-1, P]], channel_multiplier=1, waits=[zeroed], signal=const_ready)
    pool.do(G.affine_select, out=mask_rows[:, :], in_=mask_rows[:, :], compare_op=ALU.is_ge, fill=MASKED,
            base=0, pattern=[[-1, P]], channel_multiplier=1, waits=[zeroed], signal=const_ready)
    consts = pool.do(G.affine_select, out=mask_cols[:, :], in_=mask_cols[:, :], compare_op=ALU.is_ge,
                     fill=MASKED, base=0, pattern=[[1, P]], channel_multiplier=-1, waits=[zeroed],
                     signal=const_ready)

    def pool_alone(op, dst, *args, waits=(), signal=None):
        before = [(s, s.count) for s in (const_ready, pool_done, lo_pool) if s.count]
        token = pool.do(op, dst, *args, waits=[*waits, *before], signal=signal)
        pool.do(None, waits=[token])
        return token

    def statistics(b, waits):
        for t in range(TB * b, TB * b + TB):
            st = dve.do(V.bn_stats, stats[:, t, :], x[:, t, :], waits=waits, signal=dve_done)
        for t in range(TB * b, TB * b + TB):
            mv = dve.do(V.bn_aggr, meanvar[:, t, :], stats[:, t, :], waits=[st], signal=dve_done)
        sl = slice(TB * b, TB * b + TB)
        eps = pool.do(G.tensor_scalar, rstd[:, sl], meanvar[:, sl, 1], LN_EPS, None, ALU.add,
                      waits=[mv], signal=pool_done)
        return pool.do(G.tensor_tensor, rstd[:, sl], rstd[:, sl], minus_half[:, sl], ALU.pow,
                       waits=[eps], signal=pool_done)

    def normalise(dst, t, waits, **kw):
        return dve.do(V.tensor_scalar, dst, x[:, t, :], meanvar[:, t, 0:1], rstd[:, t:t + 1],
                      ALU.subtract, ALU.mult, waits=waits, signal=dve_done, **kw)

    def transposed(src, b, dst, waits, rows=BQ):
        slot, free = wide.take()
        for t in range(-(-rows // P)):
            n = min(P, rows - t * P)
            for c in range(DC):
                last = pe.do(TE.transpose, slot[:, c * BQ + t * P:c * BQ + t * P + n],
                             src[:n, t, c * P:(c + 1) * P], ident[:n, :n],
                             waits=[*waits, *free, consts], signal=pe_rows)
        done = act.do(SC.copy, dst[:, :, b * BQ:b * BQ + rows],
                      slot[:, :].rearrange("p (c t) -> p c t", c=DC)[:, :, 0:rows],
                      waits=[last], signal=act_done)
        wide.read_by(done)
        return done

    def layer_norm_transposed(b, waits, keep=None):
        ready = statistics(b, waits)
        if keep is None:
            buf, free = x_norm.take()
        else:
            buf, free = keep[:, TB * b:TB * b + TB, :], ()
        for t in range(TB):
            done = normalise(buf[:, t, :], TB * b + t, [ready, *free])
        moved = transposed(buf, b, norm_t, [done])
        if keep is None:
            x_norm.read_by(moved)
        return moved

    s1 = ExitStack()
    x_norm = Ring([sb(f"x_norm{i}", [P, TB, D], F32, s1) for i in range(2)])
    wq1 = sb("wq1", [P, DC, D], F32, s1)
    wk1 = sb("wk1", [P, DC, D], F32, s1)
    wv1 = sb("wv1", [P, DC, D], F32, s1)
    wo1 = sb("wo1", [P, DC, D], F32, s1)
    part = {(n, p): sb(f"{n}_{p}", [P, DC, T], F32R, s1) for n in "qk" for p in ("hi", "lo")}
    NSTACK = 2
    q_stack = [sb(f"q_stack{i}", [P, T], F32R, s1) for i in range(NSTACK)]
    k_stack = [sb(f"k_stack{i}", [P, T], F32R, s1) for i in range(NSTACK)]
    VW1 = 3 * DH1 + 2
    v_self = sb("v_self", [P, NT, H, VW1], BF16, s1)
    ONE1 = 2 * DH1
    v_rest = Ring([o_t.bufs[0][:, :, :].rearrange("p c t -> p (c t)").rearrange("p (t d) -> p t d", t=TB)])

    alibi = sb("alibi", [2 * H + 8, T], F32, s1)

    for b in range(NB):
        sp.do(SY.dma_start, x[:, TB * b:TB * b + TB, :],
              A["x"][0, b * BQ:(b + 1) * BQ, :].rearrange("(t p) d -> p t d", p=P), signal=x_in[b], by=16)
    for w, name in ((wq1, "wq1"), (wk1, "wk1"), (wv1, "wv1"), (wo1, "wo1")):
        w_self = sp.do(SY.dma_start, w[:, :, :], A[name].rearrange("(c p) n -> p c n", p=P),
                       signal=w_self_in, by=16)
    pad_zero = None
    for buf in (*q_stack, *k_stack):
        pad_zero = pool_alone(G.memset, buf[64:P, :].bitcast(F32), 0.0, signal=const_ready)
    alibi_loaded = sp.do(SY.dma_start, alibi[:, :], A["alibi"], signal=alibi_in, by=16)
    for i in range(NSTACK):
        r = STACKED
        for dst, src in ((q_stack[i][r:r + 3:2, :], MINUS_POS), (k_stack[i][r + 1:r + 4:2, :], POS),
                         (k_stack[i][r + 4:r + 6, :], ONES)):
            sp.do(SY.dma_start, dst.bitcast(F32), alibi[src:src + 2, :], waits=[alibi_loaded, pad_zero],
                  signal=stack_in[i], by=16)
    v_one = pool.do(G.memset, v_self[:, :, :, ONE1:ONE1 + 1], 1.0, signal=const_ready)

    qk_ready = []
    v_ready = None
    for b in range(NB):
        moved = layer_norm_transposed(b, [x_in[b].next(0)])
        tok = slice(b * BQ, (b + 1) * BQ)
        for n, w in (("q", wq1), ("k", wk1)):
            slot, free = wide.take()
            for c in range(DC):
                for kc in range(DC):
                    done = pe.do(TE.matmul, slot[:, c * BQ:(c + 1) * BQ], w[:, kc, c * P:(c + 1) * P],
                                 norm_t[:, kc, tok], start=kc == 0, stop=kc == DC - 1,
                                 waits=[moved, w_self, *free], signal=pe_rows)
            src = slot[:, :].rearrange("p (c t) -> p c t", c=DC)
            hi = act.do(SC.copy, part[n, "hi"][:, :, tok], src, waits=[done], signal=act_done)
            lo = dve.do(V.tensor_tensor, part[n, "lo"][:, :, tok], src, part[n, "hi"][:, :, tok].bitcast(F32),
                        ALU.subtract, waits=[hi], signal=dve_done)
            wide.read_by(lo)
            qk_ready = [hi, lo]
        slot, free = wide.take()
        for t in range(TB):
            for kc in range(DC):
                done = pe.do(TE.matmul, slot[:, t * D:(t + 1) * D],
                             norm_t[:, kc, (TB * b + t) * P:(TB * b + t + 1) * P], wv1[:, kc, :],
                             start=kc == 0, stop=kc == DC - 1, waits=[moved, w_self, *free], signal=pe_rows)
        rest, rest_free = v_rest.take()
        full = slot[:, :].rearrange("p (t h d) -> p t h d", t=TB, h=H)
        rest4 = rest[:, :, :].rearrange("p t (h d) -> p t h d", h=H)
        vt = v_self[:, TB * b:TB * b + TB, :, :]
        v1 = act.do(SC.copy, vt[:, :, :, 0:DH1], full, waits=[done], signal=act_done)
        r1 = dve.do(V.tensor_tensor, rest4, full, vt[:, :, :, 0:DH1], ALU.subtract,
                    waits=[v1, *rest_free], signal=dve_done)
        wide.read_by(r1)
        v2 = act.do(SC.copy, vt[:, :, :, DH1:2 * DH1], rest4, waits=[r1], signal=act_done)
        v3 = dve.do(V.tensor_tensor, vt[:, :, :, ONE1 + 1:ONE1 + 1 + DH1], rest4, vt[:, :, :, DH1:2 * DH1],
                    ALU.subtract, waits=[v2], signal=dve_done)
        v_rest.read_by(v3)
        o_t.free[0] = (v3,)
        v_ready = v3
    o_self = norm_t[:, :, :].rearrange("p c t -> p (c t)").rearrange("p (t d) -> p t d", t=NT)
    norm_t_read = done

    step_count = [0]

    def sweep1_tile(head, i, n_keys, operands, mask, waits):
        par = head % 2
        tokens = []
        for ch, k0 in enumerate(range(0, n_keys, 2 * BQ)):
            k1 = min(n_keys, k0 + 2 * BQ)
            slot, free = wide.take()
            for b0 in range(k0, k1, BQ):
                b1 = min(k1, b0 + BQ)
                wdt = b1 - b0 + (b1 - b0) % 2
                masked = mask is not None and b1 == n_keys
                for j, (q, k) in enumerate(operands):
                    done = pe.do(TE.matmul, slot[:, b0 - k0:b0 - k0 + wdt], q[:, i * P:(i + 1) * P],
                                 k[:, b0:b0 + wdt], start=j == 0, stop=j == len(operands) - 1 and not masked,
                                 waits=[*waits, *free], signal=pe_rows)
                if masked:
                    done = pe.do(TE.matmul, slot[:, n_keys - P - k0:n_keys - k0], ident_bf[:, :], mask[:, :],
                                 start=False, stop=True, waits=[consts], signal=pe_rows)
            top = dve.do(V.reduce_max, maxima[:, par, i, ch:ch + 1], slot[:, 0:k1 - k0], AX.X,
                         waits=[done, *shift_read[par]], signal=dve_max)
            wide.read_by(top)
            tokens.append(top)
        return tokens[-1]

    shift_read = [(), ()]

    def shift_rows(head, buf, top, dst_hi, dst_lo, dst_free, scale):
        par = head % 2
        neg = dve.do(V.tensor_reduce, shift[:, par, :], maxima[:, par, :, :], AX.X, ALU.max, negate=True,
                     waits=[top], signal=dve_max)
        add = dve.do(V.tensor_scalar, shift[:, par, :], shift[:, par, :],
                     float(WEIGHT_BITS * np.log(2.0) / scale), None, ALU.add, waits=[neg], signal=dve_max)
        slot, free = wide.take()
        tr = pe.do(TE.transpose, slot[0:NT, 0:P], shift[:, par, :], ident[:, :],
                   waits=[add, *free], signal=pe_rows)
        hi = act.do(SC.copy, shift_hi[:, par, :], slot[0:NT, 0:P],
                    waits=[tr, *maxrow_done[par]], signal=act_done)
        lo = dve.do(V.tensor_tensor, shift_lo[:, par, :], slot[0:NT, 0:P],
                    shift_hi[:, par, :].bitcast(F32), ALU.subtract,
                    waits=[hi, *maxrow_done[par]], signal=dve_done)
        wide.read_by(lo)
        shift_read[par] = (tr,)
        s = maxrow_in[buf]
        dst_hi, dst_lo = (r.bitcast(F32).rearrange("a (t p) -> a t p", p=P) for r in (dst_hi, dst_lo))
        sp.do(SY.dma_start, dst_hi, shift_hi[:, par, :].bitcast(F32),
              waits=[hi, *dst_free], signal=s, by=16)
        done = sp.do(SY.dma_start, dst_lo, shift_lo[:, par, :].bitcast(F32),
                     waits=[lo, *dst_free], signal=s, by=16)
        maxrow_done[par] = (done,)
        return done

    maxrow_done = [(), ()]

    def weights(step, kw, n, scale, scored):
        slot = scores.bufs[scores.at]
        i = step % len(w_hi)
        hi = act.do(SC.activation, w_hi[i][:kw, 0:n], slot[:kw, 0:n], ACT.Exp, scale=scale,
                    waits=[scored, *hi_read[i]], signal=exp_hi)
        f = step % len(w_full)
        full = act.do(SC.activation, w_full[f][:kw, 0:n], slot[:kw, 0:n], ACT.Exp, scale=scale,
                      waits=[*full_read[f]], signal=exp_full)
        scores.read_by(full)
        q, e, s = (pool, G, lo_pool) if step % POOL_EVERY == 0 and kw == P else (dve, V, lo_dve)
        lo = q.do(e.tensor_tensor, w_lo[i][:kw, 0:n], w_full[f][:kw, 0:n], w_hi[i][:kw, 0:n],
                  ALU.subtract, waits=[full, *hi_read[i]], signal=s)
        full_read[f] = (lo,)
        return i, hi, lo

    POOL_EVERY = 5
    hi_read, full_read = [()] * 4, [()] * 4

    def attend(i, hi, lo, kw, tiles, first, last, value, wide_n, narrow_n, per_bank, waits):
        nonlocal sums_free
        for t, col in tiles:
            o = sums[:, t // per_bank, (t % per_bank) * (BQ // per_bank):]
            opens = first and t % per_bank == 0
            pe.do(TE.matmul, o[:, 0:wide_n], w_hi[i][:kw, col:col + P], value[:kw, 0:wide_n],
                  start=opens, stop=False, skip_group_check=True,
                  waits=[hi, *waits, *(sums_free if first else ())])
            done = pe.do(TE.matmul, o[:, 0:narrow_n], w_lo[i][:kw, col:col + P], value[:kw, 0:narrow_n],
                         start=False, stop=last, skip_group_check=True, waits=[lo], signal=pe_values)
        hi_read[i] = (done,)
        return done

    def finish_block(par, done, per_bank, dh, dst, dst_waits):
        nonlocal sums_free
        w = 3 * dh + 1
        buf, free = o_sb.take()
        src = sums[:, :, :].rearrange("p b (k n) -> p (b k) n", k=per_bank)[:, 0:TB, 0:w] if per_bank == 2 \
            else sums[:, 0, :].rearrange("p (k n) -> p k n", k=per_bank)[:, :, 0:w]
        out_ = act.do(SC.copy, buf[:, :, 0:w], src, waits=[done, *free], signal=act_done)
        sums_free = [out_]
        inv = dve.do(V.reciprocal, recip[:, par, :], buf[:, :, 2 * dh], waits=[out_, *free], signal=dve_done)
        a = pool.do(G.tensor_tensor, buf[:, :, 0:dh], buf[:, :, 0:dh], buf[:, :, dh:2 * dh], ALU.add,
                    waits=[out_], signal=pool_done)
        a = pool.do(G.tensor_tensor, buf[:, :, 0:dh], buf[:, :, 0:dh], buf[:, :, 2 * dh + 1:3 * dh + 1],
                    ALU.add, waits=[a], signal=pool_done)
        a = pool.do(G.tensor_tensor, dst, buf[:, :, 0:dh],
                    recip[:, par, :].unsqueeze(2).broadcast_to([P, TB, dh]), ALU.mult,
                    waits=[a, inv, *dst_waits], signal=pool_done)
        o_sb.read_by(a)
        return a

    def interleave(main, side, share=0.88):
        n, m, at = len(main), len(side), 0
        for k, step in enumerate(main):
            while at < m and at * n * share < m * k + 1e-9:
                side[at]()
                at += 1
            step()
        while at < m:
            side[at]()
            at += 1

    LAG = 2

    stack_free = [[pad_zero]] * NSTACK
    stack_ready, max_ready = {}, {}
    block_out = {}

    def load_stacks(h):
        i = h % NSTACK
        c, r0 = divmod(h * DH1, P)
        for which, order, dst in (("q", ("hi", "lo", "hi", "lo"), q_stack[i]),
                                  ("k", ("hi", "hi", "lo", "lo"), k_stack[i])):
            for j, p in enumerate(order):
                sp.do(SY.dma_start, dst[j * DH1:(j + 1) * DH1, :].bitcast(F32),
                      part[which, p][r0:r0 + DH1, c, :].bitcast(F32),
                      waits=[*qk_ready, *stack_free[i]], signal=stack_in[i], by=16)
        r = STACKED
        for dst, src in ((q_stack[i][r + 1:r + 4:2, :], 2 * h), (k_stack[i][r:r + 3:2, :], 2 * h),
                         (q_stack[i][r + 4:r + 6, :], ZEROS)):
            stack_ready[h] = sp.do(SY.dma_start, dst.bitcast(F32), alibi[src:src + 2, :],
                                   waits=[*stack_free[i]], signal=stack_in[i], by=16)

    def self_sweep1(h):
        i = h % NSTACK
        state = {}

        def tile_step(t):
            state["top"] = sweep1_tile(h, t, (t + 1) * P, [(q_stack[i], k_stack[i])], mask_rows,
                                       [stack_ready[h]])
            state["pe"] = (pe_rows, pe_rows.count)

        def finish():
            max_ready[h] = shift_rows(h, i, state["top"], q_stack[i][STACKED + 4:STACKED + 5, :],
                                      q_stack[i][STACKED + 5:STACKED + 6, :],
                                      [state["pe"]], 1.0 / DH1 ** 0.5)
        return [lambda t=t: tile_step(t) for t in range(NT)] + [finish]

    def self_sweep2(h):
        i = h % NSTACK
        waiting = []
        steps = []

        def step(b, j):
            q0 = max(b * BQ, j * P)
            n = (b + 1) * BQ - q0
            slot, free = scores.take()
            diag = j >= TB * b
            scored = pe.do(TE.matmul, slot[:, 0:n], k_stack[i][:, j * P:(j + 1) * P], q_stack[i][:, q0:q0 + n],
                           start=True, stop=not diag, waits=[max_ready[h], *free], signal=pe_scores)
            if diag:
                scored = pe.do(TE.matmul, slot[:, 0:P], ident_bf[:, :], mask_cols[:, :], start=False,
                               stop=True, signal=pe_scores)
            s = step_count[0]
            step_count[0] += 1
            buf, hi, lo = weights(s, P, n, 1.0 / DH1 ** 0.5, scored)
            tiles = [(t, (TB * b + t) * P - q0) for t in range(TB) if TB * b + t >= j]
            waiting.append((b, j, buf, hi, lo, tiles))
            stack_last[i] = scored
            if len(waiting) > LAG:
                product()

        def product():
            b, j, buf, hi, lo, tiles = waiting.pop(0)
            done = attend(buf, hi, lo, P, tiles, j == 0, j == TB * b + TB - 1, v_self[:, j, h, :], 3 * DH1 + 1,
                          2 * DH1 + 1, TB, [v_ready, v_one])
            if j == TB * b + TB - 1:
                block_out[h, b] = finish_block(b % 2, done, TB, DH1,
                                               o_self[:, TB * b:TB * b + TB, h * DH1:(h + 1) * DH1],
                                               [norm_t_read])

        def drain():
            while waiting:
                product()
            stack_free[i] = [stack_last[i]]

        for b in range(NB):
            for j in range(TB * b + TB):
                steps.append(lambda b=b, j=j: step(b, j))
        steps.append(drain)
        return steps

    stack_last = {}
    load_stacks(0)
    load_stacks(1)
    for s in self_sweep1(0):
        s()
    for h in range(H):
        if h >= 1 and h + 1 < H:
            load_stacks(h + 1)
        interleave(self_sweep2(h), self_sweep1(h + 1) if h + 1 < H else [])

    def project_out(src_t, weight, n, b, waits):
        slot, free = wide.take()
        for t in range(TB):
            for kc in range(n):
                done = pe.do(TE.matmul, slot[:, t * D:(t + 1) * D], src_t[:, kc, t * P:(t + 1) * P],
                             weight[:, kc, :], start=kc == 0, stop=kc == n - 1,
                             waits=[*waits, *free], signal=pe_rows)
        return slot[:, :].rearrange("p (t d) -> p t d", t=TB), done

    x_ready = []
    for b in range(NB):
        buf, free = o_t.take()
        moved = transposed(o_self[:, TB * b:TB * b + TB, :], 0, buf, [block_out[H - 1, b], *free])
        slot, done = project_out(buf, wo1, DC, b, [moved, w_self])
        o_t.read_by(done)
        xb = x[:, TB * b:TB * b + TB, :]
        added = dve.do(V.tensor_tensor, xb, slot, xb, ALU.add, waits=[done], signal=dve_done)
        wide.read_by(added)
        x_ready.append(added)
    all_self = [(s, s.count) for s in (pe_rows, pe_scores, pe_values, act_done, exp_full, lo_dve, lo_pool,
                                       dve_max, dve_done, pool_done, *stack_in, *maxrow_in)]
    s1.close()

    resid = sb("resid", [P, NT, D], F32)
    gamma = sb("gamma", [P, D], F32)
    beta = sb("beta", [P, D], F32)
    bias8 = sb("bias8", [P, D], BF16)
    w8_raw = sb("w8_raw", [P, DC, D], BF16)
    w8 = sb("w8", [P, DC, D], BF16)
    scales = sb("scales", [P, 2], F32)
    inv_scales = sb("inv_scales", [P, 2], F32)
    out_scale = sb("out_scale", [P, 1], F32)
    s2 = ExitStack()
    wq2 = [sb(f"wq2_{i}", [P, DC, 2 * DH2], F32, s2) for i in range(2)]
    wk2 = [sb(f"wk2_{i}", [P, DC, 2 * DH2], F32, s2) for i in range(2)]
    wv2 = [sb(f"wv2_{i}", [P, DC, D], F32, s2) for i in range(2)]
    wo2 = [sb(f"wo2_{i}", [P, DC, D], F32, s2) for i in range(2)]
    q_dup = [sb(f"q_dup{i}", [P, T], F32R, s2) for i in range(2)]
    q_low = [sb(f"q_low{i}", [P, T], F32R, s2) for i in range(2)]
    k_both = [sb(f"k_both{i}", [P, SE], F32R, s2) for i in range(2)]
    k_high = [sb(f"k_high{i}", [P, SE], F32R, s2) for i in range(2)]
    HP = 2
    VW2 = 3 * DH2 + 2
    v_cross = [sb(f"v_cross{i}", [P, NS, HP, VW2], BF16, s2) for i in range(2)]
    v_part = Ring([sb("v_part", [P, TB, HP * DH2], F32, s2)])
    ONE2 = 2 * DH2
    ctx_t = sb("ctx_t", [P, DC, SE], F32, s2)
    o_cross = sb("o_cross", [P, NT, D], F32, s2)
    bq2 = sb("bq2", [P, H], F32, s2)
    bk2 = sb("bk2", [P, H], F32, s2)
    bv2 = [sb(f"bv2_{i}", [P, D], F32, s2) for i in range(2)]
    bo2 = sb("bo2", [P, D], F32, s2)
    GH = D // DH2

    def load_group(g, waits):
        i, s = g % 2, w_cross_in[g % 2]
        cols = slice(g * D, (g + 1) * D)
        sp.do(SY.dma_start, wv2[i][:, :, :], A["wv2"][:, cols].rearrange("(c p) n -> p c n", p=P),
              waits=waits, signal=s, by=16)
        sp.do(SY.dma_start, bv2[i][:, :], A["bv2"][cols].partition_broadcast(P), waits=waits, signal=s, by=16)
        return sp.do(SY.dma_start, wo2[i][:, :, :], A["wo2"][cols, :].rearrange("(c p) n -> p c n", p=P),
                     waits=waits, signal=s, by=16)

    def load_head(h, waits):
        i = h % 2
        for w, name in ((wq2, "wq2"), (wk2, "wk2")):
            for half in range(2):
                done = sp.do(SY.dma_start, w[i][:, :, half * DH2:(half + 1) * DH2],
                             A[name][:, h * DH2:(h + 1) * DH2].rearrange("(c p) n -> p c n", p=P),
                             waits=waits, signal=w_head_in[i], by=16)
        return done

    w_head_ready = {h: load_head(h, all_self) for h in range(2)}
    w_ready = {0: load_group(0, all_self), 1: load_group(1, all_self)}
    sp.do(SY.dma_start, bq2[:, :], A["bq2"], signal=small_in, by=16)
    sp.do(SY.dma_start, bk2[:, :], A["bk2"], signal=small_in, by=16)
    biases = sp.do(SY.dma_start, bo2[:, :], A["bo2"].partition_broadcast(P), signal=small_in, by=16)

    ctx_rows = o_cross
    NFULL = S // P
    sp.do(SY.dma_start, ctx_rows[:, 0:NFULL, :],
          A["ctx"][0, 0:NFULL * P, :].rearrange("(t p) d -> p t d", p=P), signal=ctx_in, by=16)
    ctx_loaded = sp.do(SY.dma_start, ctx_rows[0:S - NFULL * P, NFULL, :], A["ctx"][0, NFULL * P:S, :],
                       signal=ctx_in, by=16)
    pool.do(None, waits=all_self)
    zero_tail = pool.do(G.memset, ctx_t[:, :, S:SE], 0.0, signal=const_ready) if SE > S else None
    for i in range(2):
        pool.do(G.memset, v_cross[i][:, :, :, ONE2:ONE2 + 1], 1.0, signal=const_ready)
        pool_alone(G.memset, q_low[i][DH2:P, :].bitcast(F32), 0.0, signal=const_ready)
        pool.do(G.memset, k_both[i][:, S:SE].bitcast(F32), 0.0, signal=const_ready)
        pool_alone(G.memset, k_high[i][0:DH2, S:SE].bitcast(F32), 0.0, signal=const_ready)
        z = pool_alone(G.memset, k_high[i][DH2:P, :].bitcast(F32), 0.0, signal=const_ready)
        cross_consts = pool_alone(G.memset, k_high[i][DH2:DH2 + 2, :].bitcast(F32), 1.0, waits=[z],
                               signal=const_ready)
    act.do(None, waits=all_self)
    dve.do(None, waits=all_self)
    pe.do(None, waits=all_self)

    ctx_ready = None
    for b in range(-(-S // BQ)):
        rows = min(BQ, S - b * BQ)
        ctx_ready = transposed(ctx_rows[:, TB * b:, :], b, ctx_t, [ctx_loaded], rows)
    ctx_rows_read = (pe_rows, pe_rows.count)

    norm_ready = []
    resid_ready = []
    for b in range(NB):
        norm_ready.append(layer_norm_transposed(b, [x_ready[b]], keep=resid))
        rb = resid[:, TB * b:TB * b + TB, :]
        resid_ready.append(pool.do(G.tensor_tensor, rb, rb, bo2[:, :].unsqueeze(1).broadcast_to([P, TB, D]),
                                   ALU.add, waits=[norm_ready[b], biases], signal=pool_done))

    kv_free = [(), ()]
    v_free = [(), ()]
    operands_ready, zero_rows, v_cross_ready = {}, {}, {}

    def head_operands(h):
        i, g = h % 2, h // GH
        w = [w_head_ready[h], biases, cross_consts]
        tokens = {}

        def clear_rows():
            zero_rows[h] = pool_alone(G.memset, q_low[i][DH2:DH2 + 2, :].bitcast(F32), 0.0,
                                   waits=[*kv_free[i]], signal=pool_done)

        def queries(b):
            slot, free = wide.take()
            for half in range(2):
                c = slice((2 * b + half) * BQ, (2 * b + half + 1) * BQ)
                for kc in range(DC):
                    done = pe.do(TE.matmul, slot[:, half * BQ:(half + 1) * BQ], wq2[i][:, kc, :],
                                 norm_t[:, kc, c], start=kc == 0, stop=kc == DC - 1,
                                 waits=[*w, norm_ready[-1], *free], signal=pe_rows)
            c = slice(2 * b * BQ, 2 * (b + 1) * BQ)
            hi = act.do(SC.activation, q_dup[i][:, c], slot[:, :], ACT.Identity, bias=bq2[:, h:h + 1],
                        waits=[done, *kv_free[i]], signal=act_done)
            lo = dve.do(V.scalar_tensor_tensor, q_low[i][0:DH2, c], slot[0:DH2, :], bq2[0:DH2, h:h + 1],
                        q_dup[i][0:DH2, c].bitcast(F32), ALU.add, ALU.subtract,
                        waits=[hi, *kv_free[i]], signal=dve_done)
            wide.read_by(lo)
            tokens["q"] = (hi, lo)

        def keys(b):
            slot, free = wide.take()
            k0, k1 = 2 * b * BQ, min(S, 2 * (b + 1) * BQ)
            for b0 in range(k0, k1, BQ):
                b1 = min(k1, b0 + BQ)
                for kc in range(DC):
                    done = pe.do(TE.matmul, slot[:, b0 - k0:b1 - k0], wk2[i][:, kc, :],
                                 ctx_t[:, kc, b0:b1], start=kc == 0, stop=kc == DC - 1,
                                 waits=[*w, ctx_ready, *free], signal=pe_rows)
            n = k1 - k0
            hi = act.do(SC.activation, k_both[i][:, k0:k1], slot[:, 0:n], ACT.Identity, bias=bk2[:, h:h + 1],
                        waits=[done, *kv_free[i]], signal=act_done)
            hi2 = act.do(SC.activation, k_high[i][0:DH2, k0:k1], slot[0:DH2, 0:n], ACT.Identity,
                         bias=bk2[0:DH2, h:h + 1], waits=[*kv_free[i]], signal=act_done)
            lower = k_both[i][DH2:P, k0:k1]
            lo = dve.do(V.scalar_tensor_tensor, lower, slot[DH2:P, 0:n], bk2[DH2:P, h:h + 1],
                        lower.bitcast(F32), ALU.add, ALU.subtract, waits=[hi2], signal=dve_done)
            wide.read_by(lo)
            tokens["k"] = (hi2, lo)

        def ready():
            if h + 2 < H:
                w_head_ready[h + 2] = load_head(h + 2, [(pe_rows, pe_rows.count)])
            operands_ready[h] = [*tokens["q"], *tokens["k"], zero_rows[h], cross_consts]

        return [clear_rows, lambda: queries(0), lambda: queries(1), lambda: keys(0), lambda: keys(1), ready]

    def head_values(pair):
        i, g = pair % 2, pair * HP // GH
        c0 = (pair * HP % GH) * DH2
        wd = HP * DH2

        def tiles(t0):
            n = min(TB, NS - t0)
            slot, free = wide.take()
            for t in range(t0, t0 + n):
                kw = min(P, S - t * P)
                for kc in range(DC):
                    done = pe.do(TE.matmul, slot[:kw, (t - t0) * wd:(t - t0 + 1) * wd],
                                 ctx_t[:, kc, t * P:t * P + kw], wv2[g % 2][:, kc, c0:c0 + wd],
                                 start=kc == 0, stop=kc == DC - 1,
                                 waits=[w_ready[g], ctx_ready, *free], signal=pe_rows)
            kw = P if t0 + n < NS else (S - t0 * P if n == 1 else P)
            buf, buf_free = v_part.take()
            full = buf[:kw, 0:n, :]
            bias = bv2[g % 2][:kw, c0:c0 + wd].unsqueeze(1).broadcast_to([kw, n, wd])
            v = dve.do(V.tensor_tensor, full, slot[:kw, 0:n * wd].rearrange("p (t d) -> p t d", t=n), bias,
                       ALU.add, waits=[done, biases, *buf_free], signal=dve_done)
            wide.read_by(v)
            full = full.rearrange("p t (h d) -> p t h d", h=HP)
            vt = v_cross[i][:kw, t0:t0 + n, :, :]
            v1 = act.do(SC.copy, vt[:, :, :, 0:DH2], full, waits=[v, cross_consts, *v_free[i]], signal=act_done)
            q, e, s = (pool, G, pool_done) if kw == P else (dve, V, dve_done)
            r1 = q.do(e.tensor_tensor, full, full, vt[:, :, :, 0:DH2], ALU.subtract, waits=[v1], signal=s)
            v2 = act.do(SC.copy, vt[:, :, :, DH2:2 * DH2], full, waits=[r1], signal=act_done)
            v3 = q.do(e.tensor_tensor, vt[:, :, :, ONE2 + 1:ONE2 + 1 + DH2], full, vt[:, :, :, DH2:2 * DH2],
                      ALU.subtract, waits=[v2], signal=s)
            v_part.read_by(v3)
            v_cross_ready[pair] = v3
        return [lambda t0=t0: tiles(t0) for t0 in range(0, NS, TB)]

    CROSS_SCALE = 1.0 / DH2 ** 0.5

    def cross_sweep1(h):
        i = h % 2
        state = {}
        ops = [(q_dup[i], k_both[i]), (q_low[i], k_high[i])]

        def tile_step(t):
            state["top"] = sweep1_tile(h, t, S, ops, None, operands_ready[h])
            state["pe"] = (pe_rows, pe_rows.count)

        def finish():
            max_ready[H + h] = shift_rows(h, i, state["top"], q_low[i][DH2:DH2 + 1, :],
                                          q_low[i][DH2 + 1:DH2 + 2, :], [state["pe"]], CROSS_SCALE)
        return [lambda t=t: tile_step(t) for t in range(NT)] + [finish]

    def cross_sweep2(h):
        i, g = h % 2, h // GH
        pair = h // HP
        waiting, steps = [], []

        def step(b, j):
            kw = min(P, S - j * P)
            slot, free = scores.take()
            for n, (q, k) in enumerate([(q_dup[i], k_both[i]), (q_low[i], k_high[i])]):
                scored = pe.do(TE.matmul, slot[:kw, :], k[:, j * P:j * P + kw], q[:, b * BQ:(b + 1) * BQ],
                               start=n == 0, stop=n == 1, waits=[max_ready[H + h], *free], signal=pe_scores)
            s = step_count[0]
            step_count[0] += 1
            buf, hi, lo = weights(s, kw, BQ, CROSS_SCALE, scored)
            waiting.append((b, j, kw, buf, hi, lo))
            stack_last[i] = scored
            if len(waiting) > LAG:
                product()

        def product():
            b, j, kw, buf, hi, lo = waiting.pop(0)
            done = attend(buf, hi, lo, kw, [(t, t * P) for t in range(TB)], j == 0, j == NS - 1,
                          v_cross[pair % 2][:, j, h % HP, :], 3 * DH2 + 1, 2 * DH2 + 1, 2,
                          [v_cross_ready[pair]])
            if j == NS - 1:
                c0 = (h % GH) * DH2
                last = finish_block(b % 2, done, 2, DH2, o_cross[:, TB * b:TB * b + TB, c0:c0 + DH2],
                                    [ctx_rows_read, *o_read[b]])
                if h % GH == GH - 1:
                    group_out(g, b, last)

        def drain():
            while waiting:
                product()
            kv_free[i] = [stack_last[i]]
            if h % HP == HP - 1:
                v_free[pair % 2] = [(pe_values, pe_values.count)]
            if h % GH == GH - 1 and g + 2 < H // GH:
                w_ready[g + 2] = load_group(g + 2, [(pe_rows, pe_rows.count)])

        for b in range(NB):
            for j in range(NS):
                steps.append(lambda b=b, j=j: step(b, j))
        steps.append(drain)
        return steps

    o_read = [()] * NB

    def group_out(g, b, last):
        buf, free = o_t.take()
        moved = transposed(o_cross[:, TB * b:TB * b + TB, :], 0, buf, [last, *free])
        o_read[b] = [(pe_rows, pe_rows.count)]
        slot, done = project_out(buf, wo2[g % 2], DC, b, [moved, w_ready[g]])
        o_t.read_by(done)
        rb = resid[:, TB * b:TB * b + TB, :]
        resid_ready[b] = dve.do(V.tensor_tensor, rb, slot, rb, ALU.add, waits=[done, resid_ready[b]],
                                signal=dve_done)
        wide.read_by(resid_ready[b])

    for s in head_operands(0) + head_values(0) + cross_sweep1(0):
        s()
    for h in range(H):
        side = []
        if h + 1 < H:
            side += head_operands(h + 1)
            if (h + 1) % HP == 0:
                side += head_values((h + 1) // HP)
            side += cross_sweep1(h + 1)
        interleave(cross_sweep2(h), side)

    all_cross = [(s, s.count) for s in (pe_rows, pe_scores, pe_values, act_done, exp_full, lo_dve, lo_pool,
                                        dve_max, dve_done, pool_done)]
    s2.close()

    q_t = Ring([sb(f"q_t{i}", [P, DC, BQ], BF16) for i in range(2)])
    tails_in = sig("tails_in")
    dve.do(None, waits=all_cross)
    act.do(None, waits=all_cross)
    sp.do(SY.dma_start, gamma[:, :], A["gamma"].partition_broadcast(P), signal=tails_in, by=16)
    sp.do(SY.dma_start, beta[:, :], A["beta"].partition_broadcast(P), signal=tails_in, by=16)
    sp.do(SY.dma_start, bias8[:, :], A["bias8"].partition_broadcast(P), signal=tails_in, by=16)
    sp.do(SY.dma_start, w8_raw[:, :, :], A["w8"].rearrange("(c p) n -> p c n", p=P), signal=tails_in, by=16)
    sp.do(SY.dma_start, scales[:, 0:1], A["s_in"].partition_broadcast(P), signal=tails_in, by=16)
    tails = sp.do(SY.dma_start, scales[:, 1:2], A["s_w"].partition_broadcast(P), signal=tails_in, by=16)
    inv = dve.do(V.reciprocal, inv_scales[:, :], scales[:, :], waits=[tails], signal=dve_done)
    osc = dve.do(V.tensor_tensor, out_scale[:, :], scales[:, 0:1], scales[:, 1:2], ALU.mult, signal=dve_done)

    yb = [sb(f"quant_y{i}", [P, TB * D], F32) for i in range(1)]
    mb = [sb(f"quant_m{i}", [P, TB * D], F32) for i in range(1)]
    quant_free = [()]

    def quantise(src, n, inv_scale, dst, waits):
        y, m = yb[0][:, 0:n], mb[0][:, 0:n]
        a = dve.do(V.tensor_scalar, y, src, inv_scale, None, ALU.mult, waits=[*waits, *quant_free[0]],
                   signal=dve_done)
        e = dve.do(V.tensor_scalar, m.bitcast(mybir.dt.int32), y.bitcast(mybir.dt.int32), 0x7F800000, None,
                   ALU.bitwise_and, waits=[a], signal=dve_done)
        e = dve.do(V.tensor_scalar, m, m, FP8_MIN_NORMAL, ROUND_TO_3_BITS, ALU.max, ALU.mult, waits=[e],
                   signal=dve_done)
        a = dve.do(V.tensor_tensor, y, y, m, ALU.add, waits=[e], signal=dve_done)
        a = dve.do(V.tensor_tensor, y, y, m, ALU.subtract, waits=[a], signal=dve_done)
        e = dve.do(V.tensor_tensor, m, y, y, ALU.mult, waits=[a], signal=dve_done)
        e = dve.do(V.tensor_scalar, m, m, FP8_MAX ** 2, 3.0e38, ALU.is_gt, ALU.mult, waits=[e], signal=dve_done)
        e = dve.do(V.tensor_scalar, m, m, 3.0e38, 0.0, ALU.mult, ALU.mult, waits=[e], signal=dve_done)
        a = dve.do(V.tensor_tensor, dst, y, m, ALU.add, waits=[e], signal=dve_done)
        quant_free[0] = (a,)
        return a

    w8_ready = quantise(w8_raw[:, :, :].rearrange("p c n -> p (c n)"), DC * D, inv_scales[:, 1:2],
                        w8[:, :, :].rearrange("p c n -> p (c n)"), [inv])

    x_bf = [sb(f"x_bf{i}", [P, TB, D], BF16) for i in range(1)]
    xq = [sb(f"xq{i}", [P, TB, D], BF16) for i in range(1)]
    y_bf = [sb(f"y_bf{i}", [P, TB, D], BF16) for i in range(1)]
    xbf_free, xq_free, y_free = (), (), ()
    for b in range(NB):
        sl = slice(TB * b, TB * b + TB)
        xb = x[:, sl, :]
        rb = resid[:, sl, :]
        for t in range(TB * b, TB * b + TB):
            st = dve.do(V.bn_stats, stats[:, t, :], resid[:, t, :], waits=[resid_ready[b]], signal=dve_done)
        for t in range(TB * b, TB * b + TB):
            mv = dve.do(V.bn_aggr, meanvar[:, t, :], stats[:, t, :], waits=[st], signal=dve_done)
        eps = pool.do(G.tensor_scalar, rstd[:, sl], meanvar[:, sl, 1], LN_EPS, None, ALU.add, waits=[mv],
                      signal=pool_done)
        rs = pool.do(G.tensor_tensor, rstd[:, sl], rstd[:, sl], minus_half[:, sl], ALU.pow, waits=[eps],
                     signal=pool_done)
        for t in range(TB * b, TB * b + TB):
            nm = dve.do(V.tensor_scalar, resid[:, t, :], resid[:, t, :], meanvar[:, t, 0:1], rstd[:, t:t + 1],
                        ALU.subtract, ALU.mult, waits=[rs], signal=dve_done)
        ga = dve.do(V.tensor_tensor, rb, rb, gamma[:, :].unsqueeze(1).broadcast_to([P, TB, D]), ALU.mult,
                    waits=[nm, tails], signal=dve_done)
        be = dve.do(V.tensor_tensor, rb, rb, beta[:, :].unsqueeze(1).broadcast_to([P, TB, D]), ALU.add,
                    waits=[ga], signal=dve_done)
        xr = dve.do(V.tensor_tensor, xb, xb, rb, ALU.add, waits=[be], signal=dve_done)
        ready = statistics(b, [xr])
        for t in range(TB):
            nm = normalise(x_bf[0][:, t, :], TB * b + t, [ready, *xbf_free])
        qz = quantise(x_bf[0][:, :, :].rearrange("p t d -> p (t d)"), TB * D, inv_scales[:, 0:1],
                      xq[0][:, :, :].rearrange("p t d -> p (t d)"), [nm, inv, *xq_free])
        xbf_free = (qz,)
        slot, free = wide.take()
        half = slot[:, 0:BQ].bitcast(BF16).rearrange("p (c t) -> p c t", c=DC)
        for t in range(TB):
            for c in range(DC):
                tr = pe.do(TE.transpose, half[:, c, t * P:(t + 1) * P], xq[0][:, t, c * P:(c + 1) * P],
                           ident_bf[:, :], waits=[qz, *free], signal=pe_rows)
        xq_free = (tr,)
        buf, buf_free = q_t.take()
        mo = act.do(SC.copy, buf[:, :, :], half, waits=[tr, *buf_free], signal=act_done)
        wide.read_by(mo)
        slot, done = project_out(buf, w8, DC, b, [mo, w8_ready])
        q_t.read_by(done)
        ys = act.do(SC.activation, y_bf[0][:, :, :], slot, ACT.Copy, scale=out_scale[:, 0:1],
                    waits=[done, osc, *y_free], signal=act_done)
        wide.read_by(ys)
        yb2 = dve.do(V.tensor_tensor, y_bf[0][:, :, :], y_bf[0][:, :, :],
                     bias8[:, :].unsqueeze(1).broadcast_to([P, TB, D]), ALU.add, waits=[ys], signal=dve_done)
        xo = dve.do(V.tensor_tensor, xb, xb, y_bf[0][:, :, :], ALU.add, waits=[yb2], signal=dve_done)
        y_free = (xo,)
        end = sp.do(SY.dma_start, out[0, b * BQ:(b + 1) * BQ, :].rearrange("(t p) d -> p t d", p=P), xb,
                    waits=[xo], signal=stored, by=16)
    sp.do(None, waits=[end])

    block = ctx.enter_context(nc.Block())

    @block.tensor
    def _(e):
        pe.run(e)

    @block.scalar
    def _(e):
        act.run(e)

    @block.vector
    def _(e):
        dve.run(e)

    @block.gpsimd
    def _(e):
        pool.run(e)

    @block.sync
    def _(e):
        sp.run(e)


def kernel(x, ctx_1024, L0_attn_Wq, L0_attn_Wk, L0_attn_Wv, L0_attn_Wo, L0_xattn_Wq, L0_xattn_bq,
           L0_xattn_Wk, L0_xattn_bk, L0_xattn_Wv, L0_xattn_bv, L0_xattn_Wo, L0_xattn_bo,
           L0_xattn_ln_gamma, L0_xattn_ln_beta, L0_ffn_kernel, L0_ffn_input_scale,
           L0_ffn_kernel_scale, L0_ffn_bias):
    import concourse.bacc as bacc
    from concourse.bass_utils import run_bass_kernel_spmd

    arrays = {
        "x": x, "ctx": ctx_1024,
        "wq1": np.asarray(L0_attn_Wq).T, "wk1": np.asarray(L0_attn_Wk).T,
        "wv1": np.asarray(L0_attn_Wv).T, "wo1": np.asarray(L0_attn_Wo).T,
        "wq2": L0_xattn_Wq,  "wk2": L0_xattn_Wk, 
        "wv2": L0_xattn_Wv, "bv2": L0_xattn_bv, "wo2": L0_xattn_Wo, "bo2": L0_xattn_bo,
        "bq2": np.tile(np.asarray(L0_xattn_bq).reshape(H, DH2).T, (2, 1)),
        "bk2": np.tile(np.asarray(L0_xattn_bk).reshape(H, DH2).T, (2, 1)),
        "gamma": L0_xattn_ln_gamma, "beta": L0_xattn_ln_beta,
        "w8": L0_ffn_kernel, "s_in": L0_ffn_input_scale, "s_w": L0_ffn_kernel_scale,
        "bias8": L0_ffn_bias, "alibi": alibi_rows(),
    }
    arrays = {f"{n}_dram": np.ascontiguousarray(a) for n, a in arrays.items()}
    nc = bacc.Bacc("TRN2", target_bir_lowering=False, num_devices=1)
    ins = {n[:-5]: nc.dram_tensor(n, a.shape, mybir.dt.from_np(a.dtype), kind="ExternalInput").ap()
           for n, a in arrays.items()}
    out = nc.dram_tensor("out_dram", (1, T, D), F32, kind="ExternalOutput").ap()
    decoder(nc, ins, out)
    return run_bass_kernel_spmd(nc, [arrays], core_ids=[0]).results[0]["out_dram"]
```

```python
from contextlib import ExitStack

import numpy as np

import concourse.bass as bass
from concourse import mybir

F32, F32R = mybir.dt.float32, mybir.dt.float32r
BF16, F16 = mybir.dt.bfloat16, mybir.dt.float16
ALU, ACT, AX = mybir.AluOpType, mybir.ActivationFunctionType, mybir.AxisListType

P = 128
T, D, S = 2048, 256, 1601
NT = T // P
DC = D // P
H = 16
DH1, DH2 = D // H, 64
NS = -(-S // P)
SE = S + S % 2
BQ = 512
NB, TB = T // BQ, BQ // P
LN_EPS = 1e-5
POOL_EVERY = 2
ROWS_LAG = 3
LAG = 3
MASKED = -1.0e30
V_BITS = 13
WEIGHT_BITS = 12
FP8_MAX = 448.0
FP8_MIN_NORMAL = 2.0 ** -6
ROUND_TO_3_BITS = 1.5 * 2.0 ** 20


MINUS_POS, POS, ONES, ZEROS = 2 * H, 2 * H + 2, 2 * H + 4, 2 * H + 6
STACKED = 4 * DH1


def slopes():
    return np.asarray([2.0 ** (-8.0 * h / H) for h in range(1, H + 1)], np.float32) * np.float32(4)


def alibi_rows():
    pos = np.arange(T, dtype=np.float32)
    whole = slopes()
    hi = (whole.view(np.uint32) & np.uint32(0xFFFFF000)).view(np.float32)
    rows = np.zeros((2 * H + 8, T), np.float32)
    rows[0:2 * H:2] = hi[:, None]
    rows[1:2 * H:2] = (whole - hi)[:, None]
    rows[MINUS_POS:MINUS_POS + 2], rows[POS:POS + 2], rows[ONES:ONES + 2] = -pos, pos, 1.0
    return rows


class Signal:

    def __init__(self, sem):
        self.sem, self.count = sem, 0

    def next(self, by):
        self.count += by
        return (self, self.count)


class Queue:

    def __init__(self):
        self.items = []

    def do(self, op, *args, waits=(), signal=None, by=1, **kw):
        token = signal.next(by) if signal else None
        self.items.append((op, args, kw, [w for w in waits if w], token, by))
        return token

    def run(self, engine):
        seen = {}
        for op, args, kw, waits, token, by in self.items:
            for sig, count in waits:
                if seen.get(id(sig), 0) < count:
                    seen[id(sig)] = count
                    engine.wait_ge(sig.sem, count)
            if op is not None:
                ins = op(*args, **kw)
                if token:
                    ins.then_inc(token[0].sem, by)


class Ring:

    def __init__(self, bufs):
        self.bufs, self.free, self.at = bufs, [()] * len(bufs), -1

    def take(self):
        self.at = (self.at + 1) % len(self.bufs)
        return self.bufs[self.at], self.free[self.at]

    def read_by(self, *tokens, slot=None):
        self.free[self.at if slot is None else slot] = tokens


def decoder(nc, ins, out):
    ctx = ExitStack()
    with ctx:
        _decoder(nc, ctx, ins, out)


def _decoder(nc, ctx, A, out):
    V, SC, G, TE, SY = nc.vector, nc.scalar, nc.gpsimd, nc.tensor, nc.sync
    pe, act, dve, pool, sp = Queue(), Queue(), Queue(), Queue(), Queue()

    def sb(name, shape, dt, stack=ctx):
        return stack.enter_context(nc.sbuf_tensor(name, shape, dt))

    def sig(name):
        return Signal(ctx.enter_context(nc.semaphore(name)))

    const_ready = sig("const_ready")
    pe_rows = sig("pe_rows")
    pe_scores = sig("pe_scores")
    pe_values = sig("pe_values")
    act_done = sig("act_done")
    exp_hi = sig("exp_hi")
    exp_full = sig("exp_full")
    lo_dve = sig("lo_dve")
    lo_pool = sig("lo_pool")
    dve_max = sig("dve_max")
    dve_done = sig("dve_done")
    pool_done = sig("pool_done")
    x_in = [sig(f"x_in{i}") for i in range(2)]
    ctx_in = sig("ctx_in")
    w_self_in = sig("w_self_in")
    alibi_in = sig("alibi_in")
    small_in = sig("small_in")
    w_cross_in = [sig(f"w_cross_in{i}") for i in range(2)]
    w_pair_in = [sig(f"w_pair_in{i}") for i in range(2)]
    stack_in = [sig(f"stack_in{i}") for i in range(3)]
    maxrow_in = [[sig(f"maxrow_in{i}_{b}") for b in range(NB)] for i in range(3)]
    middle_out = sig("middle_out")
    stored = sig("stored")

    x_blocks = Ring([sb(f"x_block{i}", [P, TB, D], F32) for i in range(2)])
    ident = sb("ident", [P, P], F32)
    ident_bf = sb("ident_bf", [P, P], BF16)
    mask_rows = sb("mask_rows", [P, P], BF16)
    mask_cols = sb("mask_cols", [P, P], BF16)
    stats = sb("stats", [P, NT, 6], F32)
    meanvar = sb("meanvar", [P, NT, 2], F32)
    rstd = sb("rstd", [P, NT], F32)
    minus_half = sb("minus_half", [P, NT], F32)
    maxima = sb("maxima", [P, 2, NT, 2], F32)
    shift = sb("shift", [P, 2, NT], F32)
    shift_hi = sb("shift_hi", [TB, 2, P], F32R)
    shift_lo = sb("shift_lo", [TB, 2, P], F32R)
    w_full = [sb(f"w_full{i}", [P, BQ], F32) for i in range(4)]
    w_hi = [sb(f"w_hi{i}", [P, BQ], F16) for i in range(LAG + 2)]
    w_lo = [sb(f"w_lo{i}", [P, BQ], F16) for i in range(LAG + 2)]
    OW = 2 * DH2 + 1
    o_sb = Ring([sb(f"o_sb{i}", [P, TB, OW], F32) for i in range(2)])
    recip = sb("recip", [P, 2, TB], F32)
    norm_t = sb("norm_t", [P, DC, T], F32)
    o_t = Ring([sb("o_t", [P, DC, BQ], F32)])

    wide = Ring([ctx.enter_context(nc.psum_tensor(f"wide{i}", [P, 2 * BQ], F32)) for i in range(2)])
    scores = Ring([ctx.enter_context(nc.psum_tensor(f"scores{i}", [P, BQ], F32)) for i in range(2)])
    sums = ctx.enter_context(nc.psum_tensor("sums", [P, 2, BQ], F32))
    sums_free = []

    pool.do(G.memset, ident[:, :], 0.0, signal=const_ready)
    pool.do(G.memset, ident_bf[:, :], 0.0, signal=const_ready)
    pool.do(G.memset, mask_rows[:, :], 0.0, signal=const_ready)
    pool.do(G.memset, minus_half[:, :], -0.5, signal=const_ready)
    pool.do(G.memset, maxima[:, :, :, :], 4 * MASKED, signal=const_ready)
    zeroed = pool.do(G.memset, mask_cols[:, :], 0.0, signal=const_ready)
    for m in (ident, ident_bf):
        pool.do(G.affine_select, out=m[:, :], in_=m[:, :], compare_op=ALU.not_equal, fill=1.0, base=0,
                pattern=[[-1, P]], channel_multiplier=1, waits=[zeroed], signal=const_ready)
    pool.do(G.affine_select, out=mask_rows[:, :], in_=mask_rows[:, :], compare_op=ALU.is_ge, fill=MASKED,
            base=0, pattern=[[-1, P]], channel_multiplier=1, waits=[zeroed], signal=const_ready)
    consts = pool.do(G.affine_select, out=mask_cols[:, :], in_=mask_cols[:, :], compare_op=ALU.is_ge,
                     fill=MASKED, base=0, pattern=[[1, P]], channel_multiplier=-1, waits=[zeroed],
                     signal=const_ready)

    def pool_alone(op, dst, *args, waits=(), signal=None):
        before = [(s, s.count) for s in (const_ready, pool_done, lo_pool) if s.count]
        token = pool.do(op, dst, *args, waits=[*waits, *before], signal=signal)
        pool.do(None, waits=[token])
        return token

    def statistics(b, rows, waits):
        for t in range(TB):
            st = dve.do(V.bn_stats, stats[:, TB * b + t, :], rows[:, t, :], waits=waits, signal=dve_done)
        for t in range(TB * b, TB * b + TB):
            mv = dve.do(V.bn_aggr, meanvar[:, t, :], stats[:, t, :], waits=[st], signal=dve_done)
        sl = slice(TB * b, TB * b + TB)
        eps = pool.do(G.tensor_scalar, rstd[:, sl], meanvar[:, sl, 1], LN_EPS, None, ALU.add,
                      waits=[mv], signal=pool_done)
        return pool.do(G.tensor_tensor, rstd[:, sl], rstd[:, sl], minus_half[:, sl], ALU.pow,
                       waits=[eps], signal=pool_done)

    def normalise(dst, rows, b, waits):
        for t in range(TB):
            g = TB * b + t
            done = dve.do(V.tensor_scalar, dst[:, t, :], rows[:, t, :], meanvar[:, g, 0:1], rstd[:, g:g + 1],
                          ALU.subtract, ALU.mult, waits=waits, signal=dve_done)
        return done

    def transposed(src, b, dst, waits, rows=BQ):
        slot, free = wide.take()
        for t in range(-(-rows // P)):
            n = min(P, rows - t * P)
            for c in range(DC):
                last = pe.do(TE.transpose, slot[:, c * BQ + t * P:c * BQ + t * P + n],
                             src[:n, t, c * P:(c + 1) * P], ident[:n, :n],
                             waits=[*waits, *free, consts], signal=pe_rows)
        done = act.do(SC.copy, dst[:, :, b * BQ:b * BQ + rows],
                      slot[:, :].rearrange("p (c t) -> p c t", c=DC)[:, :, 0:rows],
                      waits=[last], signal=act_done)
        wide.read_by(done)
        return done

    def layer_norm_transposed(b, rows, buf, waits):
        ready = statistics(b, rows, waits)
        normed = normalise(buf, rows, b, [ready])
        return normed, transposed(buf, b, norm_t, [normed])

    def block_rows(dram, b):
        return dram[b * BQ:(b + 1) * BQ, :].rearrange("(t p) d -> p t d", p=P)

    def load_block(dram, b, waits=()):
        buf, free = x_blocks.take()
        slot = x_blocks.at
        return slot, buf, sp.do(SY.dma_start, buf[:, :, :], block_rows(dram, b), waits=[*waits, *free],
                                signal=x_in[slot], by=16)

    s1 = ExitStack()
    wo1 = sb("wo1", [P, DC, D], F32, s1)
    part = {(n, p): sb(f"{n}_{p}", [P, DC, T], F32R, s1) for n in "qk" for p in ("hi", "lo")}
    NSTACK = 3
    q_stack = [sb(f"q_stack{i}", [P, T], F32R, s1) for i in range(NSTACK - 1)]
    k_stack = [sb(f"k_stack{i}", [P, T], F32R, s1) for i in range(NSTACK - 1)]
    VW1 = 3 * DH1 + 2
    v_self = sb("v_self", [P, NT, H, VW1], BF16, s1)
    ONE1 = 2 * DH1
    v_rest = Ring([o_t.bufs[0][:, :, :].rearrange("p c t -> p (c t)").rearrange("p (t d) -> p t d", t=TB)])

    alibi = sb("alibi", [2 * H + 8, T], F32, s1)
    s1p = ExitStack()
    x_norm = Ring([sb(f"x_norm{i}", [P, TB, D], F32, s1p) for i in range(2)])
    wq1 = sb("wq1", [P, DC, D], F32, s1p)
    wk1 = sb("wk1", [P, DC, D], F32, s1p)
    wv1 = sb("wv1", [P, DC, D], F32, s1p)

    first_blocks = [load_block(A["x"][0], b) for b in range(2)]
    for w, name in ((wq1, "wq1"), (wk1, "wk1"), (wv1, "wv1"), (wo1, "wo1")):
        w_self = sp.do(SY.dma_start, w[:, :, :], A[name].rearrange("(c p) n -> p c n", p=P),
                       signal=w_self_in, by=16)
    alibi_loaded = sp.do(SY.dma_start, alibi[:, :], A["alibi"], signal=alibi_in, by=16)

    def fill_stack_constants(i, waits):
        for buf in (q_stack[i], k_stack[i]):
            zero = pool_alone(G.memset, buf[STACKED:P, :].bitcast(F32), 0.0, waits=waits, signal=const_ready)
        r = STACKED
        for dst, src in ((q_stack[i][r:r + 3:2, :], MINUS_POS), (k_stack[i][r + 1:r + 4:2, :], POS),
                         (k_stack[i][r + 4:r + 6, :], ONES)):
            sp.do(SY.dma_start, dst.bitcast(F32), alibi[src:src + 2, :], waits=[alibi_loaded, zero],
                  signal=stack_in[i], by=16)
        return zero

    stack_free = [[fill_stack_constants(i, ())] for i in range(NSTACK - 1)]
    v_one = pool.do(G.memset, v_self[:, :, :, ONE1:ONE1 + 1], 1.0, signal=const_ready)

    qk_ready = []
    v_ready = None
    for b in range(NB):
        x_slot, rows, loaded = first_blocks[b] if b < 2 else load_block(A["x"][0], b)
        buf, free = x_norm.take()
        normed, moved = layer_norm_transposed(b, rows, buf, [loaded, *free])
        x_blocks.read_by(normed, slot=x_slot)
        x_norm.read_by(moved)
        tok = slice(b * BQ, (b + 1) * BQ)
        for n, w in (("q", wq1), ("k", wk1)):
            slot, free = wide.take()
            for c in range(DC):
                for kc in range(DC):
                    done = pe.do(TE.matmul, slot[:, c * BQ:(c + 1) * BQ], w[:, kc, c * P:(c + 1) * P],
                                 norm_t[:, kc, tok], start=kc == 0, stop=kc == DC - 1,
                                 waits=[moved, w_self, *free], signal=pe_rows)
            src = slot[:, :].rearrange("p (c t) -> p c t", c=DC)
            hi = act.do(SC.copy, part[n, "hi"][:, :, tok], src, waits=[done], signal=act_done)
            lo = dve.do(V.tensor_tensor, part[n, "lo"][:, :, tok], src, part[n, "hi"][:, :, tok].bitcast(F32),
                        ALU.subtract, waits=[hi], signal=dve_done)
            wide.read_by(lo)
            qk_ready = [hi, lo]
        slot, free = wide.take()
        for t in range(TB):
            for kc in range(DC):
                done = pe.do(TE.matmul, slot[:, t * D:(t + 1) * D],
                             norm_t[:, kc, (TB * b + t) * P:(TB * b + t + 1) * P], wv1[:, kc, :],
                             start=kc == 0, stop=kc == DC - 1, waits=[moved, w_self, *free], signal=pe_rows)
        rest, rest_free = v_rest.take()
        full = slot[:, :].rearrange("p (t h d) -> p t h d", t=TB, h=H)
        rest4 = rest[:, :, :].rearrange("p t (h d) -> p t h d", h=H)
        vt = v_self[:, TB * b:TB * b + TB, :, :]
        v1 = act.do(SC.copy, vt[:, :, :, 0:DH1], full, waits=[done], signal=act_done)
        r1 = dve.do(V.tensor_tensor, rest4, full, vt[:, :, :, 0:DH1], ALU.subtract,
                    waits=[v1, *rest_free], signal=dve_done)
        wide.read_by(r1)
        v2 = act.do(SC.copy, vt[:, :, :, DH1:2 * DH1], rest4, waits=[r1], signal=act_done)
        v3 = dve.do(V.tensor_tensor, vt[:, :, :, ONE1 + 1:ONE1 + 1 + DH1], rest4, vt[:, :, :, DH1:2 * DH1],
                    ALU.subtract, waits=[v2], signal=dve_done)
        v_rest.read_by(v3)
        o_t.free[0] = (v3,)
        v_ready = v3
    o_self = norm_t[:, :, :].rearrange("p c t -> p (c t)").rearrange("p (t d) -> p t d", t=NT)
    norm_t_read = done

    step_count = [0]

    later = []

    def run_later(force=False):
        for item in list(later):
            item[0] -= 1
            if force or item[0] <= 0:
                later.remove(item)
                item[1]()

    maxima_read = [[()] * NB for _ in range(2)]
    maxrow_done = [(), ()]
    max_ready = {}

    def sweep1_steps(head, key, chunks, operands, mask, ready, rows, rows_sig, scale):
        par = head % 2

        def chunk(i, ch, segments, last):
            slot, free = wide.take()
            for n, (b0, b1, real) in enumerate(segments):
                at = n * BQ
                masked = mask is not None and last and n == len(segments) - 1
                for j, (q, k) in enumerate(operands):
                    done = pe.do(TE.matmul, slot[:, at:at + b1 - b0], q[:, i * P:(i + 1) * P],
                                 k[:, b0:b1], start=j == 0, stop=j == len(operands) - 1 and not masked,
                                 waits=[*ready(), *free], signal=pe_rows)
                if masked:
                    done = pe.do(TE.matmul, slot[:, at + real - P:at + real], ident_bf[:, :], mask[:, :],
                                 start=False, stop=True, waits=[consts], signal=pe_rows)
            real = {real for _, _, real in segments}
            if len(real) == 1:
                src = slot[:, :].rearrange("p (n k) -> p n k", k=BQ)[:, 0:len(segments), 0:real.pop()]
                axes = AX.XY
            else:
                src, axes = slot[:, 0:BQ + segments[1][2]], AX.X
            top = dve.do(V.tensor_reduce, maxima[:, par, i, ch:ch + 1], src, axes, ALU.max,
                         waits=[done, *maxima_read[par][i // TB]], signal=dve_max)
            wide.read_by(top)

        def negate(b):
            tiles = slice(TB * b, TB * b + TB)
            top = (dve_max, dve_max.count)
            neg = dve.do(V.tensor_reduce, shift[:, par, tiles], maxima[:, par, tiles, :], AX.X, ALU.max,
                         negate=True, waits=[top, *maxima_read[par][b]], signal=dve_max)
            add = dve.do(V.tensor_scalar, shift[:, par, tiles], shift[:, par, tiles],
                         float(WEIGHT_BITS * np.log(2.0) / scale), None, ALU.add, waits=[neg], signal=dve_max)
            scored = (pe_rows, pe_rows.count)
            return lambda: to_rows(b, add, scored)

        def to_rows(b, shifted, scored):
            slot, free = wide.take()
            tr = pe.do(TE.transpose, slot[0:TB, 0:P], shift[:, par, TB * b:TB * b + TB], ident[:, :],
                       waits=[shifted, *free], signal=pe_rows)
            hi = act.do(SC.copy, shift_hi[:, b % 2, :], slot[0:TB, 0:P],
                        waits=[tr, *maxrow_done[b % 2]], signal=act_done)
            lo = dve.do(V.tensor_tensor, shift_lo[:, b % 2, :], slot[0:TB, 0:P],
                        shift_hi[:, b % 2, :].bitcast(F32), ALU.subtract,
                        waits=[hi, *maxrow_done[b % 2]], signal=dve_done)
            wide.read_by(lo)
            maxima_read[par][b] = (tr,)
            for part, src, made in zip(rows, (shift_hi, shift_lo), (hi, lo)):
                dst = part[:, b * BQ:(b + 1) * BQ].bitcast(F32).rearrange("a (t p) -> a t p", p=P)
                done = sp.do(SY.dma_start, dst, src[:, b % 2, :].bitcast(F32), waits=[made, scored],
                             signal=rows_sig[b], by=16)
            maxrow_done[b % 2] = (done,)
            max_ready[key, b] = done

        steps, pending, made_later = [], [], []
        for i in range(NT):
            todo = chunks(i)
            for ch, segments in enumerate(todo):
                work = (sum(s[1] - s[0] for s in segments) + P) / BQ
                steps.append((work, lambda i=i, ch=ch, segments=segments, last=ch == len(todo) - 1:
                              chunk(i, ch, segments, last)))
                if pending and pending[0] == len(steps):
                    steps.append((0, lambda: made_later.pop(0)()))
                    pending.pop(0)
            if i % TB == TB - 1:
                b = i // TB
                if b < NB - 1:
                    steps.append((0, lambda b=b: made_later.append(negate(b))))
                    pending.append(len(steps) + ROWS_LAG)
                else:
                    steps.append((0, lambda b=b: later.append([ROWS_LAG, negate(b)])))
        return steps

    def weights(step, kw, n, scale, scored):
        slot = scores.bufs[scores.at]
        i = step % len(w_hi)
        hi = act.do(SC.activation, w_hi[i][:kw, 0:n], slot[:kw, 0:n], ACT.Exp, scale=scale,
                    waits=[scored, *hi_read[i]], signal=exp_hi)
        f = step % len(w_full)
        full = act.do(SC.activation, w_full[f][:kw, 0:n], slot[:kw, 0:n], ACT.Exp, scale=scale,
                      waits=[*full_read[f]], signal=exp_full)
        scores.read_by(full)
        q, e, s = (pool, G, lo_pool) if step % POOL_EVERY == 0 and kw == P else (dve, V, lo_dve)
        lo = q.do(e.tensor_tensor, w_lo[i][:kw, 0:n], w_full[f][:kw, 0:n], w_hi[i][:kw, 0:n],
                  ALU.subtract, waits=[full, *hi_read[i]], signal=s)
        full_read[f] = (lo,)
        return i, hi, lo

    hi_read, full_read = [()] * len(w_hi), [()] * len(w_full)

    def attend(i, hi, lo, kw, tiles, first, last, value, wide_n, narrow_n, per_bank, waits):
        nonlocal sums_free
        for t, col in tiles:
            o = sums[:, t // per_bank, (t % per_bank) * (BQ // per_bank):]
            opens = first and t % per_bank == 0
            pe.do(TE.matmul, o[:, 0:wide_n], w_hi[i][:kw, col:col + P], value[:kw, 0:wide_n],
                  start=opens, stop=False, skip_group_check=True,
                  waits=[hi, *waits, *(sums_free if first else ())])
            done = pe.do(TE.matmul, o[:, 0:narrow_n], w_lo[i][:kw, col:col + P], value[:kw, 0:narrow_n],
                         start=False, stop=last, skip_group_check=True, waits=[lo], signal=pe_values)
        hi_read[i] = (done,)
        return done

    def finish_block(par, done, per_bank, dh, parts, dst, dst_waits, unscale=None):
        nonlocal sums_free
        w = len(parts) * dh + 1
        one = parts[-1] - 1
        buf, free = o_sb.take()
        src = sums[:, :, :].rearrange("p b (k n) -> p (b k) n", k=per_bank)[:, 0:TB, 0:w] if per_bank == 2 \
            else sums[:, 0, :].rearrange("p (k n) -> p k n", k=per_bank)[:, :, 0:w]
        out_ = act.do(SC.copy, buf[:, :, 0:w], src, waits=[done, *free], signal=act_done)
        sums_free = [out_]
        inv = dve.do(V.reciprocal, recip[:, par, :], buf[:, :, one], waits=[out_, *free], signal=dve_done)
        if unscale is not None:
            inv = dve.do(V.tensor_scalar, recip[:, par, :], recip[:, par, :], unscale, None, ALU.mult,
                         waits=[inv], signal=dve_done)
        a = out_
        for part in parts[1:]:
            a = pool.do(G.tensor_tensor, buf[:, :, 0:dh], buf[:, :, 0:dh], buf[:, :, part:part + dh], ALU.add,
                        waits=[a], signal=pool_done)
        a = pool.do(G.tensor_tensor, dst, buf[:, :, 0:dh],
                    recip[:, par, :].unsqueeze(2).broadcast_to([P, TB, dh]), ALU.mult,
                    waits=[a, inv, *dst_waits], signal=pool_done)
        o_sb.read_by(a)
        return a

    def interleave(main, side, start=0.0, end=0.9):
        whole, side_whole = sum(w for w, _ in main), sum(w for w, _ in side) or 1
        at, done, side_done = 0, 0, 0
        for work, step in main:
            while at < len(side) and start + (end - start) * side_done / side_whole <= done / whole:
                side_done += side[at][0]
                side[at][1]()
                at += 1
            step()
            done += work
        for _, step in side[at:]:
            step()


    s1p.close()
    q_stack.append(sb(f"q_stack{NSTACK - 1}", [P, T], F32R, s1))
    k_stack.append(sb(f"k_stack{NSTACK - 1}", [P, T], F32R, s1))
    projected = [(g, g.count) for g in (pe_rows, act_done, dve_done)]
    stack_free.append([fill_stack_constants(NSTACK - 1, projected), *projected])
    stack_ready = {}
    block_out = {}

    def load_stacks(h):
        i = h % NSTACK
        c, r0 = divmod(h * DH1, P)
        for which, order, dst in (("q", ("hi", "lo", "hi", "lo"), q_stack[i]),
                                  ("k", ("hi", "hi", "lo", "lo"), k_stack[i])):
            for j, p in enumerate(order):
                sp.do(SY.dma_start, dst[j * DH1:(j + 1) * DH1, :].bitcast(F32),
                      part[which, p][r0:r0 + DH1, c, :].bitcast(F32),
                      waits=[*qk_ready, *stack_free[i]], signal=stack_in[i], by=16)
        r = STACKED
        for dst, src in ((q_stack[i][r + 1:r + 4:2, :], 2 * h), (k_stack[i][r:r + 3:2, :], 2 * h),
                         (q_stack[i][r + 4:r + 6, :], ZEROS)):
            stack_ready[h] = sp.do(SY.dma_start, dst.bitcast(F32), alibi[src:src + 2, :],
                                   waits=[*stack_free[i]], signal=stack_in[i], by=16)

    def self_sweep1(h):
        i = h % NSTACK

        def chunks(tile):
            n = (tile + 1) * P
            segments = [(k0, min(n, k0 + BQ), min(n, k0 + BQ) - k0) for k0 in range(0, n, BQ)]
            return [segments[c:c + 2] for c in range(0, len(segments), 2)]

        r = STACKED + 4
        return sweep1_steps(h, h, chunks, [(q_stack[i], k_stack[i])], mask_rows, lambda: [stack_ready[h]],
                            (q_stack[i][r:r + 1, :], q_stack[i][r + 1:r + 2, :]), maxrow_in[i],
                            1.0 / DH1 ** 0.5)

    def self_sweep2(h):
        i = h % NSTACK
        waiting = []
        steps = []

        def step(b, j):
            q0 = max(b * BQ, j * P)
            n = (b + 1) * BQ - q0
            slot, free = scores.take()
            diag = j >= TB * b
            scored = pe.do(TE.matmul, slot[:, 0:n], k_stack[i][:, j * P:(j + 1) * P], q_stack[i][:, q0:q0 + n],
                           start=True, stop=not diag, waits=[max_ready[h, b], *free], signal=pe_scores)
            if diag:
                scored = pe.do(TE.matmul, slot[:, 0:P], ident_bf[:, :], mask_cols[:, :], start=False,
                               stop=True, signal=pe_scores)
            s = step_count[0]
            step_count[0] += 1
            buf, hi, lo = weights(s, P, n, 1.0 / DH1 ** 0.5, scored)
            tiles = [(t, (TB * b + t) * P - q0) for t in range(TB) if TB * b + t >= j]
            waiting.append((b, j, buf, hi, lo, tiles))
            stack_last[i] = scored
            if len(waiting) > LAG:
                product()
            run_later()

        def product():
            b, j, buf, hi, lo, tiles = waiting.pop(0)
            done = attend(buf, hi, lo, P, tiles, j == 0, j == TB * b + TB - 1, v_self[:, j, h, :], 3 * DH1 + 1,
                          2 * DH1 + 1, TB, [v_ready, v_one])
            if j == TB * b + TB - 1:
                block_out[h, b] = finish_block(b % 2, done, TB, DH1, (0, DH1, 2 * DH1 + 1),
                                               o_self[:, TB * b:TB * b + TB, h * DH1:(h + 1) * DH1],
                                               [norm_t_read])

        def drain():
            while waiting:
                product()
            stack_free[i] = [stack_last[i]]

        for b in range(NB):
            for j in range(TB * b + TB):
                steps.append((min(TB, TB * b + TB - j) + 1, lambda b=b, j=j: step(b, j)))
        steps.append((1, drain))
        return steps

    stack_last = {}
    load_stacks(0)
    load_stacks(1)
    for _, s in self_sweep1(0):
        s()
    run_later(force=True)
    for h in range(H):
        if h + 2 < H:
            load_stacks(h + 2)
        interleave(self_sweep2(h), self_sweep1(h + 1) if h + 1 < H else [], start=0.0, end=0.92)

    def project_out(src_t, weight, n, b, waits):
        slot, free = wide.take()
        for t in range(TB):
            for kc in range(n):
                done = pe.do(TE.matmul, slot[:, t * D:(t + 1) * D], src_t[:, kc, t * P:(t + 1) * P],
                             weight[:, kc, :], start=kc == 0, stop=kc == n - 1,
                             waits=[*waits, *free], signal=pe_rows)
        return slot[:, :].rearrange("p (t d) -> p t d", t=TB), done

    def project_self(b, rows, loaded):
        buf, free = o_t.take()
        moved = transposed(o_self[:, TB * b:TB * b + TB, :], 0, buf, [block_out[H - 1, b], *free])
        slot, done = project_out(buf, wo1, DC, b, [moved, w_self])
        o_t.read_by(done)
        added = dve.do(V.tensor_tensor, rows, slot, rows, ALU.add, waits=[done, loaded], signal=dve_done)
        wide.read_by(added)
        return added

    middle = nc.dram_tensor("x_middle", (T, D), F32, kind="Internal").ap()
    for b in range(NB):
        x_slot, rows, loaded = load_block(A["x"][0], b)
        added = project_self(b, rows[:, :, :], loaded)
        middle_stored = sp.do(SY.dma_start, block_rows(middle, b), rows[:, :, :], waits=[added],
                              signal=middle_out, by=16)
        x_blocks.read_by(middle_stored)
    all_self = [(s, s.count) for s in (pe_rows, pe_scores, pe_values, act_done, exp_full, lo_dve, lo_pool,
                                       dve_max, dve_done, pool_done, *stack_in, *(s for row in maxrow_in for s in row))]
    s1.close()

    resid = sb("resid", [P, NT, D], F32)
    s2 = ExitStack()
    wq2 = [sb(f"wq2_{i}", [P, DC, P], F32, s2) for i in range(2)]
    wk2 = [sb(f"wk2_{i}", [P, DC, P], F32, s2) for i in range(2)]
    q_pair = sb("q_pair", [P, T], F32, s2)
    k_pair = sb("k_pair", [P, SE], F32, s2)
    wv2 = [sb(f"wv2_{i}", [P, DC, D], F32, s2) for i in range(2)]
    wo2 = [sb(f"wo2_{i}", [P, DC, D], F32, s2) for i in range(2)]
    q_dup = [sb(f"q_dup{i}", [P, T], F32R, s2) for i in range(2)]
    q_low = [sb(f"q_low{i}", [P, T], F32R, s2) for i in range(2)]
    k_both = [sb(f"k_both{i}", [P, SE], F32R, s2) for i in range(2)]
    k_high = [sb(f"k_high{i}", [P, SE], F32R, s2) for i in range(2)]
    HP = 2
    VW2 = 2 * DH2 + 2
    v_cross = [sb(f"v_cross{i}", [P, NS, HP, VW2], F16, s2) for i in range(2)]
    v_pair = sb("v_pair", [P, NS, HP * DH2], F32, s2)
    v_top = sb("v_top", [P, 2], F32, s2)
    v_power = sb("v_power", [P, 2], F32, s2)
    v_scale = sb("v_scale", [P, 2], F32, s2)
    v_unscale = sb("v_unscale", [P, 2], F32, s2)
    ONE2 = DH2
    ctx_t = sb("ctx_t", [P, DC, SE], F32, s2)
    o_cross = sb("o_cross", [P, NT, D], F32, s2)
    bq2 = sb("bq2", [P, H // HP], F32, s2)
    bk2 = sb("bk2", [P, H // HP], F32, s2)
    bv2 = [sb(f"bv2_{i}", [P, D], F32, s2) for i in range(2)]
    bo2 = sb("bo2", [P, D], F32, s2)
    GH = D // DH2

    def load_group(g, waits):
        i, s = g % 2, w_cross_in[g % 2]
        cols = slice(g * D, (g + 1) * D)
        sp.do(SY.dma_start, wv2[i][:, :, :], A["wv2"][:, cols].rearrange("(c p) n -> p c n", p=P),
              waits=waits, signal=s, by=16)
        sp.do(SY.dma_start, bv2[i][:, :], A["bv2"][cols].partition_broadcast(P), waits=waits, signal=s, by=16)
        return sp.do(SY.dma_start, wo2[i][:, :, :], A["wo2"][cols, :].rearrange("(c p) n -> p c n", p=P),
                     waits=waits, signal=s, by=16)

    def load_pair(p, waits):
        for w, name in ((wq2, "wq2"), (wk2, "wk2")):
            done = sp.do(SY.dma_start, w[p % 2][:, :, :],
                         A[name][:, p * P:(p + 1) * P].rearrange("(c p) n -> p c n", p=P),
                         waits=waits, signal=w_pair_in[p % 2], by=16)
        return done

    w_pair_ready = {p: load_pair(p, all_self) for p in range(2)}
    w_ready = {0: load_group(0, all_self), 1: load_group(1, all_self)}
    sp.do(SY.dma_start, bq2[:, :], A["bq2"], signal=small_in, by=16)
    sp.do(SY.dma_start, bk2[:, :], A["bk2"], signal=small_in, by=16)
    biases = sp.do(SY.dma_start, bo2[:, :], A["bo2"].partition_broadcast(P), signal=small_in, by=16)

    ctx_rows = o_cross
    NFULL = S // P
    sp.do(SY.dma_start, ctx_rows[:, 0:NFULL, :],
          A["ctx"][0, 0:NFULL * P, :].rearrange("(t p) d -> p t d", p=P), signal=ctx_in, by=16)
    ctx_loaded = sp.do(SY.dma_start, ctx_rows[0:S - NFULL * P, NFULL, :], A["ctx"][0, NFULL * P:S, :],
                       signal=ctx_in, by=16)
    pool.do(None, waits=all_self)
    zero_tail = pool.do(G.memset, ctx_t[:, :, S:SE], 0.0, signal=const_ready) if SE > S else None
    pool.do(G.memset, v_pair[:, NS - 1, :], 0.0, signal=const_ready)
    for i in range(2):
        pool.do(G.memset, v_cross[i][:, :, :, ONE2:ONE2 + 1], 1.0, signal=const_ready)
        pool_alone(G.memset, q_low[i][DH2:P, :].bitcast(F32), 0.0, signal=const_ready)
        pool.do(G.memset, k_both[i][:, S:SE].bitcast(F32), 0.0, signal=const_ready)
        pool_alone(G.memset, k_high[i][0:DH2, S:SE].bitcast(F32), 0.0, signal=const_ready)
        z = pool_alone(G.memset, k_high[i][DH2:P, :].bitcast(F32), 0.0, signal=const_ready)
        cross_consts = pool_alone(G.memset, k_high[i][DH2:DH2 + 2, :].bitcast(F32), 1.0, waits=[z],
                               signal=const_ready)
    act.do(None, waits=all_self)
    dve.do(None, waits=all_self)
    pe.do(None, waits=all_self)

    ctx_ready = None
    for b in range(-(-S // BQ)):
        rows = min(BQ, S - b * BQ)
        ctx_ready = transposed(ctx_rows[:, TB * b:, :], b, ctx_t, [ctx_loaded], rows)
    ctx_rows_read = (pe_rows, pe_rows.count)

    norm_ready = []
    resid_ready = []
    for b in range(NB):
        x_slot, rows, loaded = load_block(middle, b, [middle_stored])
        rb = resid[:, TB * b:TB * b + TB, :]
        normed, moved = layer_norm_transposed(b, rows, rb, [loaded])
        x_blocks.read_by(normed)
        norm_ready.append(moved)
        resid_ready.append(pool.do(G.tensor_tensor, rb, rb, bo2[:, :].unsqueeze(1).broadcast_to([P, TB, D]),
                                   ALU.add, waits=[moved, biases], signal=pool_done))

    kv_free = [(), ()]
    v_free = [(), ()]
    operands_ready, v_cross_ready = {}, {}

    pair_free, pair_ready = [()], {}

    def project_pair(p):
        tokens = []

        def project(w, bias, src, src_ready, dst, b, n):
            slot, free = wide.take()
            k0, k1 = 2 * b * BQ, min(n, 2 * (b + 1) * BQ)
            for b0 in range(k0, k1, BQ):
                b1 = min(k1, b0 + BQ)
                for kc in range(DC):
                    done = pe.do(TE.matmul, slot[:, b0 - k0:b1 - k0], w[p % 2][:, kc, :], src[:, kc, b0:b1],
                                 start=kc == 0, stop=kc == DC - 1,
                                 waits=[w_pair_ready[p], *src_ready, *free], signal=pe_rows)
            out_ = act.do(SC.activation, dst[:, k0:k1], slot[:, 0:k1 - k0], ACT.Identity, bias=bias[:, p:p + 1],
                          waits=[done, biases, *pair_free[0]], signal=act_done)
            wide.read_by(out_)
            tokens.append(out_)

        def end():
            pair_ready[p] = tokens[-1]
            if p + 2 < H // HP:
                w_pair_ready[p + 2] = load_pair(p + 2, [(pe_rows, pe_rows.count)])

        return [(7, lambda b=b: project(wq2, bq2, norm_t, norm_ready, q_pair, b, T)) for b in range(2)] \
            + [(7, lambda b=b: project(wk2, bk2, ctx_t, [ctx_ready], k_pair, b, S)) for b in range(2)] \
            + [(0, end)]

    def head_operands(h):
        i, r = h % 2, (h % HP) * DH2
        mine, low, high = slice(r, r + DH2), slice(0, DH2), slice(DH2, P)
        tokens = []

        def clear_rows():
            tokens.append(pool_alone(G.memset, q_low[i][DH2:DH2 + 2, :].bitcast(F32), 0.0,
                                     waits=[*kv_free[i]], signal=pool_done))

        def queries(b):
            c = slice(2 * b * BQ, 2 * (b + 1) * BQ)
            w = [pair_ready[h // HP], *kv_free[i]]
            hi_low = act.do(SC.copy, q_dup[i][low, c], q_pair[mine, c], waits=w, signal=act_done)
            hi_high = dve.do(V.tensor_copy, q_dup[i][high, c], q_pair[mine, c], waits=w, signal=dve_done)
            lo = dve.do(V.tensor_tensor, q_low[i][low, c], q_pair[mine, c], q_dup[i][mine, c].bitcast(F32),
                        ALU.subtract, waits=[hi_low, hi_high, cross_consts], signal=dve_done)
            tokens.extend((hi_low, lo))

        def keys():
            c = slice(0, S)
            w = [pair_ready[h // HP], *kv_free[i]]
            hi = act.do(SC.copy, k_high[i][low, c], k_pair[mine, c], waits=[*w, cross_consts], signal=act_done)
            own = dve.do(V.tensor_copy, k_both[i][mine, c], k_pair[mine, c], waits=w, signal=dve_done)
            lo = dve.do(V.tensor_tensor, k_both[i][high, c], k_pair[mine, c], k_both[i][mine, c].bitcast(F32),
                        ALU.subtract, waits=[own], signal=dve_done)
            tokens.extend((hi, lo))
            if r:
                tokens.append(act.do(SC.copy, k_both[i][low, c], k_pair[mine, c], signal=act_done))

        def ready():
            operands_ready[h] = [*tokens, cross_consts]
            pair_free[0] = tuple(tokens)

        return [(0, clear_rows), (2, lambda: queries(0)), (2, lambda: queries(1)), (2, keys), (0, ready)]

    v_pair_free = [()]

    def head_values(pair):
        i, g = pair % 2, pair * HP // GH
        c0 = (pair * HP % GH) * DH2
        wd = HP * DH2
        tokens = []

        def tiles(t0):
            n = min(2 * TB, NS - t0)
            slot, free = wide.take()
            for t in range(t0, t0 + n):
                kw = min(P, S - t * P)
                for kc in range(DC):
                    done = pe.do(TE.matmul, slot[:kw, (t - t0) * wd:(t - t0 + 1) * wd],
                                 ctx_t[:, kc, t * P:t * P + kw], wv2[g % 2][:, kc, c0:c0 + wd],
                                 start=kc == 0, stop=kc == DC - 1,
                                 waits=[w_ready[g], ctx_ready, *free], signal=pe_rows)
            for kw, ta, tb in ((P, t0, min(t0 + n, NFULL)), (S - NFULL * P, NFULL, t0 + n)):
                if ta < tb:
                    bias = bv2[g % 2][:kw, c0:c0 + wd].unsqueeze(1).broadcast_to([kw, tb - ta, wd])
                    src = slot[:kw, (ta - t0) * wd:(tb - t0) * wd].rearrange("p (t d) -> p t d", d=wd)
                    v = dve.do(V.tensor_tensor, v_pair[:kw, ta:tb, :], src, bias, ALU.add,
                               waits=[done, *v_pair_free[0], cross_consts], signal=dve_done)
            wide.read_by(v)
            tokens.append(v)

        def split():
            top = dve.do(V.tensor_reduce, v_top[:, 0:1], v_pair[:, :, :], AX.XY, ALU.max,
                         apply_absolute_value=True, waits=[tokens[-1], *v_pair_free[0]], signal=dve_done)
            top = pool.do(G.partition_all_reduce, v_top[:, 1:2], v_top[:, 0:1], P, bass.bass_isa.ReduceOp.max,
                          waits=[top], signal=pool_done)
            pw, sc, un = (v[:, i:i + 1] for v in (v_power, v_scale, v_unscale))
            e = dve.do(V.tensor_scalar, pw, v_top[:, 1:2], 2.0 ** -100, None, ALU.max,
                       waits=[top, *v_free[i]], signal=dve_done)
            e = dve.do(V.tensor_scalar, pw.bitcast(mybir.dt.int32), pw.bitcast(mybir.dt.int32), 0x7F800000,
                       None, ALU.bitwise_and, waits=[e], signal=dve_done)
            e = dve.do(V.tensor_scalar, un, pw, 2.0 ** -V_BITS, None, ALU.mult,
                       waits=[e, *v_free[i]], signal=dve_done)
            e = dve.do(V.reciprocal, sc, un, waits=[e, *v_free[i]], signal=dve_done)
            full = v_pair[:, :, :].rearrange("p t (h d) -> p t h d", h=HP)
            for ta, tb in ((0, NS // 2), (NS // 2, NS)):
                hi = v_cross[i][:, ta:tb, :, 0:DH2]
                h_ = act.do(SC.activation, hi, full[:, ta:tb], ACT.Copy, scale=sc,
                            waits=[e, cross_consts, *v_free[i]], signal=act_done)
                v_cross_ready[pair] = dve.do(V.scalar_tensor_tensor,
                                             v_cross[i][:, ta:tb, :, ONE2 + 1:ONE2 + 1 + DH2],
                                             full[:, ta:tb], sc, hi, ALU.mult, ALU.subtract,
                                             waits=[h_, *v_free[i]], signal=dve_done)
            v_pair_free[0] = (v_cross_ready[pair],)

        return [(6, lambda t0=t0: tiles(t0)) for t0 in range(0, NS, 2 * TB)] + [(4, split)]

    CROSS_SCALE = 1.0 / DH2 ** 0.5

    def cross_sweep1(h):
        i = h % 2
        return sweep1_steps(h, H + h, lambda tile: CROSS_CHUNKS, [(q_dup[i], k_both[i]), (q_low[i], k_high[i])],
                            None, lambda: operands_ready[h],
                            (q_low[i][DH2:DH2 + 1, :], q_low[i][DH2 + 1:DH2 + 2, :]), maxrow_in[i], CROSS_SCALE)

    QUARTER = (SE // 4) // 2 * 2
    LAST = S - 2 * QUARTER - (S - 2 * QUARTER) // 2
    LAST_AT = (S - LAST) // 2 * 2
    LAST = S - LAST_AT
    CROSS_CHUNKS = [[(0, QUARTER, QUARTER), (QUARTER, 2 * QUARTER, QUARTER)],
                    [(2 * QUARTER, 2 * QUARTER + LAST + LAST % 2, LAST), (LAST_AT, LAST_AT + LAST + LAST % 2, LAST)]]

    def cross_sweep2(h):
        i, g = h % 2, h // GH
        pair = h // HP
        waiting, steps = [], []

        def step(b, j):
            kw = min(P, S - j * P)
            slot, free = scores.take()
            for n, (q, k) in enumerate([(q_dup[i], k_both[i]), (q_low[i], k_high[i])]):
                scored = pe.do(TE.matmul, slot[:kw, :], k[:, j * P:j * P + kw], q[:, b * BQ:(b + 1) * BQ],
                               start=n == 0, stop=n == 1, waits=[max_ready[H + h, b], *free], signal=pe_scores)
            s = step_count[0]
            step_count[0] += 1
            buf, hi, lo = weights(s, kw, BQ, CROSS_SCALE, scored)
            waiting.append((b, j, kw, buf, hi, lo))
            stack_last[i] = scored
            if len(waiting) > LAG:
                product()
            run_later()

        def product():
            b, j, kw, buf, hi, lo = waiting.pop(0)
            done = attend(buf, hi, lo, kw, [(t, t * P) for t in range(TB)], j == 0, j == NS - 1,
                          v_cross[pair % 2][:, j, h % HP, :], 2 * DH2 + 1, DH2 + 1, 2,
                          [v_cross_ready[pair]])
            if j == NS - 1:
                c0 = (h % GH) * DH2
                last = finish_block(b % 2, done, 2, DH2, (0, DH2 + 1),
                                    o_cross[:, TB * b:TB * b + TB, c0:c0 + DH2],
                                    [ctx_rows_read, *o_read[b]], v_unscale[:, pair % 2:pair % 2 + 1])
                unscaled[pair % 2] = (dve_done, dve_done.count)
                if h % GH == GH - 1:
                    group_out(g, b, last)

        def drain():
            while waiting:
                product()
            kv_free[i] = [stack_last[i]]
            if h % HP == HP - 1:
                v_free[pair % 2] = [(pe_values, pe_values.count), unscaled[pair % 2]]

        for b in range(NB):
            for j in range(NS):
                steps.append((TB, lambda b=b, j=j: step(b, j)))
        steps.append((1, drain))
        return steps

    o_read = [()] * NB
    unscaled = {}

    def group_out(g, b, last):
        buf, free = o_t.take()

        def turn():
            moved = transposed(o_cross[:, TB * b:TB * b + TB, :], 0, buf, [last, *free])
            o_read[b] = [(pe_rows, pe_rows.count)]
            later.append([2, lambda: project(moved)])

        def project(moved):
            slot, done = project_out(buf, wo2[g % 2], DC, b, [moved, w_ready[g]])
            o_t.read_by(done)
            rb = resid[:, TB * b:TB * b + TB, :]
            resid_ready[b] = dve.do(V.tensor_tensor, rb, slot, rb, ALU.add, waits=[done, resid_ready[b]],
                                    signal=dve_done)
            wide.read_by(resid_ready[b])
            if b == NB - 1 and g + 2 < H // GH:
                w_ready[g + 2] = load_group(g + 2, [(pe_rows, pe_rows.count)])

        later.append([3, turn])

    for _, s in project_pair(0) + head_operands(0) + head_values(0) + cross_sweep1(0):
        s()
    run_later(force=True)
    for h in range(H):
        side = []
        if h + 1 < H:
            if (h + 1) % HP == 0:
                side += project_pair((h + 1) // HP)
            side += head_operands(h + 1)
            if (h + 1) % HP == 0:
                side += head_values((h + 1) // HP)
            side += cross_sweep1(h + 1)
        interleave(cross_sweep2(h), side)
    while later:
        run_later(force=True)

    all_cross = [(s, s.count) for s in (pe_rows, pe_scores, pe_values, act_done, exp_full, lo_dve, lo_pool,
                                        dve_max, dve_done, pool_done)]
    s2.close()

    gamma = sb("gamma", [P, D], F32)
    beta = sb("beta", [P, D], F32)
    bias8 = sb("bias8", [P, D], BF16)
    w8_raw = sb("w8_raw", [P, DC, D], BF16)
    w8 = sb("w8", [P, DC, D], BF16)
    scales = sb("scales", [P, 2], F32)
    inv_scales = sb("inv_scales", [P, 2], F32)
    out_scale = sb("out_scale", [P, 1], F32)
    q_t = Ring([sb(f"q_t{i}", [P, DC, BQ], BF16) for i in range(2)])
    tails_in = sig("tails_in")
    dve.do(None, waits=all_cross)
    act.do(None, waits=all_cross)
    sp.do(None, waits=all_cross)
    sp.do(SY.dma_start, gamma[:, :], A["gamma"].partition_broadcast(P), signal=tails_in, by=16)
    sp.do(SY.dma_start, beta[:, :], A["beta"].partition_broadcast(P), signal=tails_in, by=16)
    sp.do(SY.dma_start, bias8[:, :], A["bias8"].partition_broadcast(P), signal=tails_in, by=16)
    sp.do(SY.dma_start, w8_raw[:, :, :], A["w8"].rearrange("(c p) n -> p c n", p=P), signal=tails_in, by=16)
    sp.do(SY.dma_start, scales[:, 0:1], A["s_in"].partition_broadcast(P), signal=tails_in, by=16)
    tails = sp.do(SY.dma_start, scales[:, 1:2], A["s_w"].partition_broadcast(P), signal=tails_in, by=16)
    inv = dve.do(V.reciprocal, inv_scales[:, :], scales[:, :], waits=[tails], signal=dve_done)
    osc = dve.do(V.tensor_tensor, out_scale[:, :], scales[:, 0:1], scales[:, 1:2], ALU.mult, signal=dve_done)

    yb = [sb(f"quant_y{i}", [P, TB * D], F32) for i in range(1)]
    mb = [sb(f"quant_m{i}", [P, TB * D], F32) for i in range(1)]
    quant_free = [()]

    def quantise(src, n, inv_scale, dst, waits):
        y, m = yb[0][:, 0:n], mb[0][:, 0:n]
        a = dve.do(V.tensor_scalar, y, src, inv_scale, None, ALU.mult, waits=[*waits, *quant_free[0]],
                   signal=dve_done)
        e = dve.do(V.tensor_scalar, m.bitcast(mybir.dt.int32), y.bitcast(mybir.dt.int32), 0x7F800000, None,
                   ALU.bitwise_and, waits=[a], signal=dve_done)
        e = dve.do(V.tensor_scalar, m, m, FP8_MIN_NORMAL, ROUND_TO_3_BITS, ALU.max, ALU.mult, waits=[e],
                   signal=dve_done)
        a = dve.do(V.tensor_tensor, y, y, m, ALU.add, waits=[e], signal=dve_done)
        a = dve.do(V.tensor_tensor, y, y, m, ALU.subtract, waits=[a], signal=dve_done)
        e = dve.do(V.tensor_tensor, m, y, y, ALU.mult, waits=[a], signal=dve_done)
        e = dve.do(V.tensor_scalar, m, m, FP8_MAX ** 2, 3.0e38, ALU.is_gt, ALU.mult, waits=[e], signal=dve_done)
        e = dve.do(V.tensor_scalar, m, m, 3.0e38, 0.0, ALU.mult, ALU.mult, waits=[e], signal=dve_done)
        a = dve.do(V.tensor_tensor, dst, y, m, ALU.add, waits=[e], signal=dve_done)
        quant_free[0] = (a,)
        return a

    w8_ready = quantise(w8_raw[:, :, :].rearrange("p c n -> p (c n)"), DC * D, inv_scales[:, 1:2],
                        w8[:, :, :].rearrange("p c n -> p (c n)"), [inv])

    x_bf = [sb(f"x_bf{i}", [P, TB, D], BF16) for i in range(1)]
    xq = [sb(f"xq{i}", [P, TB, D], BF16) for i in range(1)]
    y_bf = [sb(f"y_bf{i}", [P, TB, D], BF16) for i in range(1)]
    xbf_free, xq_free, y_free = (), (), ()
    for b in range(NB):
        sl = slice(TB * b, TB * b + TB)
        x_slot, xb, loaded = load_block(middle, b)
        rb = resid[:, sl, :]
        rs = statistics(b, rb, [resid_ready[b]])
        nm = normalise(rb, rb, b, [rs])
        ga = dve.do(V.tensor_tensor, rb, rb, gamma[:, :].unsqueeze(1).broadcast_to([P, TB, D]), ALU.mult,
                    waits=[nm, tails], signal=dve_done)
        be = dve.do(V.tensor_tensor, rb, rb, beta[:, :].unsqueeze(1).broadcast_to([P, TB, D]), ALU.add,
                    waits=[ga], signal=dve_done)
        xr = dve.do(V.tensor_tensor, xb[:, :, :], xb[:, :, :], rb, ALU.add, waits=[be, loaded], signal=dve_done)
        ready = statistics(b, xb, [xr])
        nm = normalise(x_bf[0], xb, b, [ready, *xbf_free])
        qz = quantise(x_bf[0][:, :, :].rearrange("p t d -> p (t d)"), TB * D, inv_scales[:, 0:1],
                      xq[0][:, :, :].rearrange("p t d -> p (t d)"), [nm, inv, *xq_free])
        xbf_free = (qz,)
        slot, free = wide.take()
        half = slot[:, 0:BQ].bitcast(BF16).rearrange("p (c t) -> p c t", c=DC)
        for t in range(TB):
            for c in range(DC):
                tr = pe.do(TE.transpose, half[:, c, t * P:(t + 1) * P], xq[0][:, t, c * P:(c + 1) * P],
                           ident_bf[:, :], waits=[qz, *free], signal=pe_rows)
        xq_free = (tr,)
        buf, buf_free = q_t.take()
        mo = act.do(SC.copy, buf[:, :, :], half, waits=[tr, *buf_free], signal=act_done)
        wide.read_by(mo)
        slot, done = project_out(buf, w8, DC, b, [mo, w8_ready])
        q_t.read_by(done)
        ys = act.do(SC.activation, y_bf[0][:, :, :], slot, ACT.Copy, scale=out_scale[:, 0:1],
                    waits=[done, osc, *y_free], signal=act_done)
        wide.read_by(ys)
        yb2 = dve.do(V.tensor_tensor, y_bf[0][:, :, :], y_bf[0][:, :, :],
                     bias8[:, :].unsqueeze(1).broadcast_to([P, TB, D]), ALU.add, waits=[ys], signal=dve_done)
        xo = dve.do(V.tensor_tensor, xb[:, :, :], xb[:, :, :], y_bf[0][:, :, :], ALU.add, waits=[yb2], signal=dve_done)
        y_free = (xo,)
        end = sp.do(SY.dma_start, block_rows(out[0], b), xb[:, :, :], waits=[xo], signal=stored, by=16)
        x_blocks.read_by(end, slot=x_slot)
    sp.do(None, waits=[end])

    block = ctx.enter_context(nc.Block())

    @block.tensor
    def _(e):
        pe.run(e)

    @block.scalar
    def _(e):
        act.run(e)

    @block.vector
    def _(e):
        dve.run(e)

    @block.gpsimd
    def _(e):
        pool.run(e)

    @block.sync
    def _(e):
        sp.run(e)


def kernel(x, ctx_1024, L0_attn_Wq, L0_attn_Wk, L0_attn_Wv, L0_attn_Wo, L0_xattn_Wq, L0_xattn_bq,
           L0_xattn_Wk, L0_xattn_bk, L0_xattn_Wv, L0_xattn_bv, L0_xattn_Wo, L0_xattn_bo,
           L0_xattn_ln_gamma, L0_xattn_ln_beta, L0_ffn_kernel, L0_ffn_input_scale,
           L0_ffn_kernel_scale, L0_ffn_bias):
    import concourse.bacc as bacc
    from concourse.bass_utils import run_bass_kernel_spmd

    arrays = {
        "x": x, "ctx": ctx_1024,
        "wq1": np.asarray(L0_attn_Wq).T, "wk1": np.asarray(L0_attn_Wk).T,
        "wv1": np.asarray(L0_attn_Wv).T, "wo1": np.asarray(L0_attn_Wo).T,
        "wq2": L0_xattn_Wq, "wk2": L0_xattn_Wk,
        "wv2": L0_xattn_Wv, "bv2": L0_xattn_bv, "wo2": L0_xattn_Wo, "bo2": L0_xattn_bo,
        "bq2": np.asarray(L0_xattn_bq).reshape(-1, P).T, "bk2": np.asarray(L0_xattn_bk).reshape(-1, P).T,
        "gamma": L0_xattn_ln_gamma, "beta": L0_xattn_ln_beta,
        "w8": L0_ffn_kernel, "s_in": L0_ffn_input_scale, "s_w": L0_ffn_kernel_scale,
        "bias8": L0_ffn_bias, "alibi": alibi_rows(),
    }
    arrays = {f"{n}_dram": np.ascontiguousarray(a) for n, a in arrays.items()}
    nc = bacc.Bacc("TRN2", target_bir_lowering=False, num_devices=1)
    ins = {n[:-5]: nc.dram_tensor(n, a.shape, mybir.dt.from_np(a.dtype), kind="ExternalInput").ap()
           for n, a in arrays.items()}
    out = nc.dram_tensor("out_dram", (1, T, D), F32, kind="ExternalOutput").ap()
    decoder(nc, ins, out)
    return run_bass_kernel_spmd(nc, [arrays], core_ids=[0]).results[0]["out_dram"]
```

```python
from contextlib import ExitStack

import numpy as np

import concourse.bass as bass
from concourse import mybir

F32, F32R = mybir.dt.float32, mybir.dt.float32r
BF16, F16 = mybir.dt.bfloat16, mybir.dt.float16
ALU, ACT, AX = mybir.AluOpType, mybir.ActivationFunctionType, mybir.AxisListType

P = 128
T, D, S = 2048, 256, 1601
NT = T // P
DC = D // P
H = 16
DH1, DH2 = D // H, 64
NS, NFULL = -(-S // P), S // P
SE = S + S % 2
BQ = 512
NB, TB = T // BQ, BQ // P
LN_EPS = 1e-5
POOL_EVERY = 2
OPERANDS_LAG = 8
ROWS_LAG = 3
TAIL_AT, TAIL_APART = (1, 4, 7, 10, 13, 15, 17), 3
LAG = 4
MASKED = -1.0e30
V_BITS = 13
WEIGHT_BITS = 12
FP8_MAX = 448.0
FP8_MIN_NORMAL = 2.0 ** -6
ROUND_TO_3_BITS = 1.5 * 2.0 ** 20


MINUS_POS, POS, ONES, ZEROS = 2 * H, 2 * H + 2, 2 * H + 4, 2 * H + 6
STACKED = 4 * DH1


def slopes():
    return np.asarray([2.0 ** (-8.0 * h / H) for h in range(1, H + 1)], np.float32) * np.float32(4)


def alibi_rows():
    pos = np.arange(T, dtype=np.float32)
    whole = slopes()
    hi = (whole.view(np.uint32) & np.uint32(0xFFFFF000)).view(np.float32)
    rows = np.zeros((2 * H + 8, T), np.float32)
    rows[0:2 * H:2] = hi[:, None]
    rows[1:2 * H:2] = (whole - hi)[:, None]
    rows[MINUS_POS:MINUS_POS + 2], rows[POS:POS + 2], rows[ONES:ONES + 2] = -pos, pos, 1.0
    return rows


class Signal:

    def __init__(self, sem):
        self.sem, self.count = sem, 0

    def next(self, by):
        self.count += by
        return (self, self.count)


class Queue:

    def __init__(self):
        self.items = []

    def do(self, op, *args, waits=(), signal=None, by=1, **kw):
        token = signal.next(by) if signal else None
        self.items.append((op, args, kw, [w for w in waits if w], token, by))
        return token

    def run(self, engine):
        seen = {}
        for op, args, kw, waits, token, by in self.items:
            for sig, count in waits:
                if seen.get(id(sig), 0) < count:
                    seen[id(sig)] = count
                    engine.wait_ge(sig.sem, count)
            if op is not None:
                ins = op(*args, **kw)
                if token:
                    ins.then_inc(token[0].sem, by)


class Ring:

    def __init__(self, bufs):
        self.bufs, self.free, self.at = bufs, [()] * len(bufs), -1

    def take(self):
        self.at = (self.at + 1) % len(self.bufs)
        return self.bufs[self.at], self.free[self.at]

    def read_by(self, *tokens, slot=None):
        self.free[self.at if slot is None else slot] = tokens


class Room:

    def __init__(self, nc, sb, name, size):
        self.nc, self.name, self.size, self.count = nc, name, size, 0
        slab = sb(name, [P, size // 4], F32)
        self.first = nc.sbuf_base - size
        self.at = 0

    def take(self, shape, dt):
        buf = self.nc.alloc_sbuf_tensor_at(f"{self.name}_{self.count}", [P, *shape], dt,
                                           offset=self.first + self.at)
        self.count += 1
        self.at += -(-int(np.prod(shape)) * mybir.dt.size(dt) // 32) * 32
        assert self.at <= self.size
        return buf[(slice(None),) * (len(shape) + 1)]

    def empty(self):
        self.at = 0
        return self


def decoder(nc, ins, out):
    ctx = ExitStack()
    with ctx:
        _decoder(nc, ctx, ins, out)


def _decoder(nc, ctx, A, out):
    V, SC, G, TE, SY = nc.vector, nc.scalar, nc.gpsimd, nc.tensor, nc.sync
    pe, act, dve, pool, sp = Queue(), Queue(), Queue(), Queue(), Queue()

    def sb(name, shape, dt, stack=ctx):
        return stack.enter_context(nc.sbuf_tensor(name, shape, dt))

    def sig(name):
        return Signal(ctx.enter_context(nc.semaphore(name)))

    const_ready = sig("const_ready")
    pe_rows = sig("pe_rows")
    pe_scores = sig("pe_scores")
    pe_values = sig("pe_values")
    act_done = sig("act_done")
    exp_hi = sig("exp_hi")
    exp_full = sig("exp_full")
    lo_dve = sig("lo_dve")
    lo_pool = sig("lo_pool")
    dve_max = sig("dve_max")
    dve_done = sig("dve_done")
    pool_done = sig("pool_done")
    x_in = [sig(f"x_in{i}") for i in range(2)]
    ctx_in = sig("ctx_in")
    w_self_in = sig("w_self_in")
    alibi_in = sig("alibi_in")
    small_in = sig("small_in")
    w_cross_in = [sig(f"w_cross_in{i}") for i in range(2)]
    w_pair_in = [sig(f"w_pair_in{i}") for i in range(2)]
    stack_in = [sig(f"stack_in{i}") for i in range(3)]
    maxrow_in = [[sig(f"maxrow_in{i}_{b}") for b in range(NB)] for i in range(3)]
    middle_out = [sig(f"middle_out{i}") for i in range(2)]
    stored = [sig(f"stored{i}") for i in range(2)]
    tails_in = sig("tails_in")

    x_blocks = Ring([sb(f"x_block{i}", [P, TB, D], F32) for i in range(2)])
    ident = sb("ident", [P, P], F32)
    ident_bf = sb("ident_bf", [P, P], BF16)
    mask_rows = sb("mask_rows", [P, P], BF16)
    mask_cols = sb("mask_cols", [P, P], BF16)
    stats = sb("stats", [P, NT, 6], F32)
    meanvar = sb("meanvar", [P, NT, 2], F32)
    rstd = sb("rstd", [P, NT], F32)
    minus_half = sb("minus_half", [P, NT], F32)
    maxima = sb("maxima", [P, 2, NT, 2], F32)
    shift = sb("shift", [P, 2, NT], F32)
    shift_hi = sb("shift_hi", [TB, 2, P], F32R)
    shift_lo = sb("shift_lo", [TB, 2, P], F32R)
    w_full = [sb(f"w_full{i}", [P, BQ], F32) for i in range(4)]
    w_hi = [sb(f"w_hi{i}", [P, BQ], F16) for i in range(LAG + 2)]
    w_lo = [sb(f"w_lo{i}", [P, BQ], F16) for i in range(LAG + 2)]
    o_sb = Ring([sb(f"o_sb{i}", [P, TB, 2 * DH2 + 1], F32) for i in range(2)])
    recip = sb("recip", [P, 2, TB], F32)
    norm_room = Room(nc, sb, "norm_room", DC * T * 4)
    norm_t = norm_room.take([DC, T], F32)
    o_t = Ring([sb("o_t", [P, DC, BQ], F32)])

    wide = Ring([ctx.enter_context(nc.psum_tensor(f"wide{i}", [P, 2 * BQ], F32)) for i in range(2)])
    scores = Ring([ctx.enter_context(nc.psum_tensor(f"scores{i}", [P, BQ], F32)) for i in range(2)])
    sums = ctx.enter_context(nc.psum_tensor("sums", [P, 2, BQ], F32))
    sums_free = []

    pool.do(G.memset, ident[:, :], 0.0, signal=const_ready)
    pool.do(G.memset, ident_bf[:, :], 0.0, signal=const_ready)
    pool.do(G.memset, mask_rows[:, :], 0.0, signal=const_ready)
    pool.do(G.memset, minus_half[:, :], -0.5, signal=const_ready)
    pool.do(G.memset, maxima[:, :, :, :], 4 * MASKED, signal=const_ready)
    zeroed = pool.do(G.memset, mask_cols[:, :], 0.0, signal=const_ready)
    for m in (ident, ident_bf):
        pool.do(G.affine_select, out=m[:, :], in_=m[:, :], compare_op=ALU.not_equal, fill=1.0, base=0,
                pattern=[[-1, P]], channel_multiplier=1, waits=[zeroed], signal=const_ready)
    pool.do(G.affine_select, out=mask_rows[:, :], in_=mask_rows[:, :], compare_op=ALU.is_ge, fill=MASKED,
            base=0, pattern=[[-1, P]], channel_multiplier=1, waits=[zeroed], signal=const_ready)
    consts = pool.do(G.affine_select, out=mask_cols[:, :], in_=mask_cols[:, :], compare_op=ALU.is_ge,
                     fill=MASKED, base=0, pattern=[[1, P]], channel_multiplier=-1, waits=[zeroed],
                     signal=const_ready)

    def pool_alone(op, dst, *args, waits=(), signal=None):
        before = [(s, s.count) for s in (const_ready, pool_done, lo_pool) if s.count]
        token = pool.do(op, dst, *args, waits=[*waits, *before], signal=signal)
        pool.do(None, waits=[token])
        return token

    def statistics(tiles, rows, first, waits):
        for n, t in enumerate(tiles):
            st = dve.do(V.bn_stats, stats[:, t, :], rows[:, first + n, :], waits=waits, signal=dve_done)
        for t in tiles:
            mv = dve.do(V.bn_aggr, meanvar[:, t, :], stats[:, t, :], waits=[st], signal=dve_done)
        sl = slice(tiles[0], tiles[-1] + 1)
        eps = pool.do(G.tensor_scalar, rstd[:, sl], meanvar[:, sl, 1], LN_EPS, None, ALU.add,
                      waits=[mv], signal=pool_done)
        return pool.do(G.tensor_tensor, rstd[:, sl], rstd[:, sl], minus_half[:, sl], ALU.pow,
                       waits=[eps], signal=pool_done)

    def normalise(dst, rows, b, waits):
        for t in range(TB):
            g = TB * b + t
            done = dve.do(V.tensor_scalar, dst[:, t, :], rows[:, t, :], meanvar[:, g, 0:1], rstd[:, g:g + 1],
                          ALU.subtract, ALU.mult, waits=waits, signal=dve_done)
        return done

    def transposed(src, b, dst, waits, rows=BQ):
        slot, free = wide.take()
        for t in range(-(-rows // P)):
            n = min(P, rows - t * P)
            for c in range(DC):
                last = pe.do(TE.transpose, slot[:, c * BQ + t * P:c * BQ + t * P + n],
                             src[:n, t, c * P:(c + 1) * P], ident[:n, :n],
                             waits=[*waits, *free, consts], signal=pe_rows)
        done = act.do(SC.copy, dst[:, :, b * BQ:b * BQ + rows],
                      slot[:, :].rearrange("p (c t) -> p c t", c=DC)[:, :, 0:rows],
                      waits=[last], signal=act_done)
        wide.read_by(done)
        return done

    def block_rows(dram, b):
        return dram[b * BQ:(b + 1) * BQ, :].rearrange("(t p) d -> p t d", p=P)

    def load_block(dram, b, waits=()):
        buf, free = x_blocks.take()
        slot = x_blocks.at
        return slot, buf, sp.do(SY.dma_start, buf[:, :, :], block_rows(dram, b), waits=[*waits, *free],
                                signal=x_in[slot], by=16)

    parts_room = Room(nc, sb, "parts_room", 4 * DC * T * 4)
    NSTACK = 3
    stack_rooms = [Room(nc, sb, f"stack_room{i}", 2 * T * 4) for i in range(NSTACK)]
    s1 = ExitStack()
    wo1 = sb("wo1", [P, DC, D], F32, s1)
    part = {(n, p): parts_room.take([DC, T], F32R) for n in "qk" for p in ("hi", "lo")}
    projection_room = stack_rooms[-1]
    x_norm = Ring([projection_room.take([TB, D], F32) for i in range(2)])
    wq1, wk1, wv1 = (projection_room.take([DC, D], F32) for _ in range(3))
    projection_room.empty()
    q_stack, k_stack = zip(*[(room.take([T], F32R), room.take([T], F32R)) for room in stack_rooms])
    VW1 = 3 * DH1 + 2
    v_self = sb("v_self", [P, NT, H, VW1], BF16, s1)
    ONE1 = 2 * DH1
    v_rest = Ring([o_t.bufs[0][:, :, :].rearrange("p c t -> p (c t)").rearrange("p (t d) -> p t d", t=TB)])

    alibi = sb("alibi", [2 * H + 8, T], F32, s1)

    first_blocks = [load_block(A["x"][0], b) for b in range(2)]
    for w, name in ((wq1, "wq1"), (wk1, "wk1"), (wv1, "wv1"), (wo1, "wo1")):
        w_self = sp.do(SY.dma_start, w[:, :, :], A[name].rearrange("(c p) n -> p c n", p=P),
                       signal=w_self_in, by=16)
    alibi_loaded = sp.do(SY.dma_start, alibi[:, :], A["alibi"], signal=alibi_in, by=16)

    def fill_stack_constants(i, waits):
        for buf in (q_stack[i], k_stack[i]):
            zero = pool_alone(G.memset, buf[STACKED:P, :].bitcast(F32), 0.0, waits=waits, signal=const_ready)
        r = STACKED
        for dst, src in ((q_stack[i][r:r + 3:2, :], MINUS_POS), (k_stack[i][r + 1:r + 4:2, :], POS),
                         (k_stack[i][r + 4:r + 6, :], ONES)):
            sp.do(SY.dma_start, dst.bitcast(F32), alibi[src:src + 2, :], waits=[alibi_loaded, zero],
                  signal=stack_in[i], by=16)
        return zero

    qk_ready, normed_t = [], {}

    def norm_block(b):
        x_slot, rows, loaded = first_blocks[b] if b < 2 else load_block(A["x"][0], b)
        buf, free = x_norm.take()
        ready = statistics(range(TB * b, TB * b + TB), rows, 0, [loaded, *free])
        normed = normalise(buf, rows, b, [ready])
        x_blocks.read_by(normed, slot=x_slot)
        return x_norm.at, buf, normed

    def turn_block(b, slot, buf, normed):
        normed_t[b] = transposed(buf, b, norm_t, [normed])
        x_norm.read_by((pe_rows, pe_rows.count), slot=slot)

    def queries_keys(b):
        tok = slice(b * BQ, (b + 1) * BQ)
        for n, w in (("q", wq1), ("k", wk1)):
            slot, free = wide.take()
            for c in range(DC):
                for kc in range(DC):
                    done = pe.do(TE.matmul, slot[:, c * BQ:(c + 1) * BQ], w[:, kc, c * P:(c + 1) * P],
                                 norm_t[:, kc, tok], start=kc == 0, stop=kc == DC - 1,
                                 waits=[normed_t[b], w_self, *free], signal=pe_rows)
            src = slot[:, :].rearrange("p (c t) -> p c t", c=DC)
            hi = act.do(SC.copy, part[n, "hi"][:, :, tok], src, waits=[done], signal=act_done)
            lo = dve.do(V.tensor_tensor, part[n, "lo"][:, :, tok], src, part[n, "hi"][:, :, tok].bitcast(F32),
                        ALU.subtract, waits=[hi], signal=dve_done)
            wide.read_by(lo)
            qk_ready[:] = [hi, lo]

    def values(b):
        slot, free = wide.take()
        for t in range(TB):
            for kc in range(DC):
                done = pe.do(TE.matmul, slot[:, t * D:(t + 1) * D],
                             norm_t[:, kc, (TB * b + t) * P:(TB * b + t + 1) * P], wv1[:, kc, :],
                             start=kc == 0, stop=kc == DC - 1, waits=[normed_t[b], w_self, *free],
                             signal=pe_rows)
        rest, rest_free = v_rest.take()
        full = slot[:, :].rearrange("p (t h d) -> p t h d", t=TB, h=H)
        rest4 = rest[:, :, :].rearrange("p t (h d) -> p t h d", h=H)
        vt = v_self[:, TB * b:TB * b + TB, :, :]
        v1 = act.do(SC.copy, vt[:, :, :, 0:DH1], full, waits=[done], signal=act_done)
        r1 = dve.do(V.tensor_tensor, rest4, full, vt[:, :, :, 0:DH1], ALU.subtract,
                    waits=[v1, *rest_free], signal=dve_done)
        wide.read_by(r1)
        v2 = act.do(SC.copy, vt[:, :, :, DH1:2 * DH1], rest4, waits=[r1], signal=act_done)
        v3 = dve.do(V.tensor_tensor, vt[:, :, :, ONE1 + 1:ONE1 + 1 + DH1], rest4, vt[:, :, :, DH1:2 * DH1],
                    ALU.subtract, waits=[v2], signal=dve_done)
        v_rest.read_by(v3)
        o_t.free[0] = (v3,)
        return done, v3

    turn_block(0, *norm_block(0))
    stack_free = [[fill_stack_constants(i, ())] for i in range(NSTACK - 1)]
    v_one = pool.do(G.memset, v_self[:, :, :, ONE1:ONE1 + 1], 1.0, signal=const_ready)
    stack_ready = {}

    def load_stacks(h):
        i = h % NSTACK
        c, r0 = divmod(h * DH1, P)
        for which, order, dst in (("q", ("hi", "lo", "hi", "lo"), q_stack[i]),
                                  ("k", ("hi", "hi", "lo", "lo"), k_stack[i])):
            for j, p in enumerate(order):
                sp.do(SY.dma_start, dst[j * DH1:(j + 1) * DH1, :].bitcast(F32),
                      part[which, p][r0:r0 + DH1, c, :].bitcast(F32),
                      waits=[*qk_ready, *stack_free[i]], signal=stack_in[i], by=16)
        r = STACKED
        for dst, src in ((q_stack[i][r + 1:r + 4:2, :], 2 * h), (k_stack[i][r:r + 3:2, :], 2 * h),
                         (q_stack[i][r + 4:r + 6, :], ZEROS)):
            stack_ready[h] = sp.do(SY.dma_start, dst.bitcast(F32), alibi[src:src + 2, :],
                                   waits=[*stack_free[i]], signal=stack_in[i], by=16)

    for b in range(NB):
        ahead = norm_block(b + 1) if b + 1 < NB else None
        queries_keys(b)
        if ahead:
            turn_block(b + 1, *ahead)
            if b:
                values(b - 1)
    load_stacks(0)
    for b in (NB - 2, NB - 1):
        done, v_ready = values(b)
    o_self = norm_t[:, :, :].rearrange("p c t -> p (c t)").rearrange("p (t d) -> p t d", t=NT)
    norm_t_read = done

    step_count = [0]

    later = []

    def run_later(force=False):
        for item in list(later):
            item[0] -= 1
            if force or item[0] <= 0:
                later.remove(item)
                item[1]()

    maxima_read = [[()] * NB for _ in range(2)]
    maxrow_done = [(), ()]
    max_ready = {}

    def sweep1_steps(head, key, chunks, operands, mask, ready, rows, rows_sig, scale,
                     at_once=False):
        par = head % 2

        def chunk(i, ch, segments, last):
            slot, free = wide.take()
            for n, (b0, b1, real) in enumerate(segments):
                at = n * BQ
                masked = mask is not None and last and n == len(segments) - 1
                for j, (q, k) in enumerate(operands):
                    done = pe.do(TE.matmul, slot[:, at:at + b1 - b0], q[:, i * P:(i + 1) * P],
                                 k[:, b0:b1], start=j == 0, stop=j == len(operands) - 1 and not masked,
                                 waits=[*ready(), *free], signal=pe_rows)
                if masked:
                    done = pe.do(TE.matmul, slot[:, at + real - P:at + real], ident_bf[:, :], mask[:, :],
                                 start=False, stop=True, waits=[consts], signal=pe_rows)
            real = {real for _, _, real in segments}
            if len(real) == 1:
                src = slot[:, :].rearrange("p (n k) -> p n k", k=BQ)[:, 0:len(segments), 0:real.pop()]
                axes = AX.XY
            else:
                src, axes = slot[:, 0:BQ + segments[1][2]], AX.X
            top = dve.do(V.tensor_reduce, maxima[:, par, i, ch:ch + 1], src, axes, ALU.max,
                         waits=[done, *maxima_read[par][i // TB]], signal=dve_max)
            wide.read_by(top)

        def negate(b):
            tiles = slice(TB * b, TB * b + TB)
            top = (dve_max, dve_max.count)
            neg = dve.do(V.tensor_reduce, shift[:, par, tiles], maxima[:, par, tiles, :], AX.X, ALU.max,
                         negate=True, waits=[top, *maxima_read[par][b]], signal=dve_max)
            add = dve.do(V.tensor_scalar, shift[:, par, tiles], shift[:, par, tiles],
                         float(WEIGHT_BITS * np.log(2.0) / scale), None, ALU.add, waits=[neg], signal=dve_max)
            scored = (pe_rows, pe_rows.count)
            return lambda: to_rows(b, add, scored)

        def to_rows(b, shifted, scored):
            slot, free = wide.take()
            tr = pe.do(TE.transpose, slot[0:TB, 0:P], shift[:, par, TB * b:TB * b + TB], ident[:, :],
                       waits=[shifted, *free], signal=pe_rows)
            hi = act.do(SC.copy, shift_hi[:, b % 2, :], slot[0:TB, 0:P],
                        waits=[tr, *maxrow_done[b % 2]], signal=act_done)
            lo = dve.do(V.tensor_tensor, shift_lo[:, b % 2, :], slot[0:TB, 0:P],
                        shift_hi[:, b % 2, :].bitcast(F32), ALU.subtract,
                        waits=[hi, *maxrow_done[b % 2]], signal=dve_done)
            wide.read_by(lo)
            maxima_read[par][b] = (tr,)
            for part, src, made in zip(rows, (shift_hi, shift_lo), (hi, lo)):
                dst = part[:, b * BQ:(b + 1) * BQ].bitcast(F32).rearrange("a (t p) -> a t p", p=P)
                done = sp.do(SY.dma_start, dst, src[:, b % 2, :].bitcast(F32), waits=[made, scored],
                             signal=rows_sig[b], by=16)
            maxrow_done[b % 2] = (done,)
            max_ready[key, b] = done

        steps, pending, made_later, ends = [], [], [], [0]
        for i in range(NT):
            todo = chunks(i)
            for ch, segments in enumerate(todo):
                work = (sum(s[1] - s[0] for s in segments) + P) / BQ
                steps.append((work, lambda i=i, ch=ch, segments=segments, last=ch == len(todo) - 1:
                              chunk(i, ch, segments, last)))
                if pending and pending[0] == len(steps):
                    steps.append((0, lambda: made_later.pop(0)()))
                    pending.pop(0)
            if i % TB == TB - 1:
                b = i // TB
                if at_once:
                    steps.append((0, lambda b=b: negate(b)()))
                    ends.append(len(steps))
                elif b < NB - 1:
                    steps.append((0, lambda b=b: made_later.append(negate(b))))
                    pending.append(len(steps) + ROWS_LAG)
                else:
                    steps.append((0, lambda b=b: later.append([ROWS_LAG, negate(b)])))
        if at_once:
            return [steps[e0:e1] for e0, e1 in zip(ends, ends[1:])]
        return steps

    def weights(step, kw, n, scale, scored):
        slot = scores.bufs[scores.at]
        i = step % len(w_hi)
        hi = act.do(SC.activation, w_hi[i][:kw, 0:n], slot[:kw, 0:n], ACT.Exp, scale=scale,
                    waits=[scored, *hi_read[i]], signal=exp_hi)
        f = step % len(w_full)
        full = act.do(SC.activation, w_full[f][:kw, 0:n], slot[:kw, 0:n], ACT.Exp, scale=scale,
                      waits=[*full_read[f]], signal=exp_full)
        scores.read_by(full)
        q, e, s = (pool, G, lo_pool) if step % POOL_EVERY == 0 and kw == P else (dve, V, lo_dve)
        lo = q.do(e.tensor_tensor, w_lo[i][:kw, 0:n], w_full[f][:kw, 0:n], w_hi[i][:kw, 0:n],
                  ALU.subtract, waits=[full, *hi_read[i]], signal=s)
        full_read[f] = (lo,)
        return i, hi, lo

    hi_read, full_read = [()] * len(w_hi), [()] * len(w_full)

    def attend(i, hi, lo, kw, tiles, first, last, value, wide_n, narrow_n, per_bank, waits):
        nonlocal sums_free
        for t, col in tiles:
            o = sums[:, t // per_bank, (t % per_bank) * (BQ // per_bank):]
            opens = first and t % per_bank == 0
            pe.do(TE.matmul, o[:, 0:wide_n], w_hi[i][:kw, col:col + P], value[:kw, 0:wide_n],
                  start=opens, stop=False, skip_group_check=True,
                  waits=[hi, *waits, *(sums_free if first else ())])
            done = pe.do(TE.matmul, o[:, 0:narrow_n], w_lo[i][:kw, col:col + P], value[:kw, 0:narrow_n],
                         start=False, stop=last, skip_group_check=True, waits=[lo], signal=pe_values)
        hi_read[i] = (done,)
        return done

    def finish_block(par, done, per_bank, dh, parts, dst, dst_waits, unscale=None):
        nonlocal sums_free
        w = len(parts) * dh + 1
        one = parts[-1] - 1
        buf, free = o_sb.take()
        src = sums[:, :, :].rearrange("p b (k n) -> p (b k) n", k=per_bank)[:, 0:TB, 0:w] if per_bank == 2 \
            else sums[:, 0, :].rearrange("p (k n) -> p k n", k=per_bank)[:, :, 0:w]
        out_ = act.do(SC.copy, buf[:, :, 0:w], src, waits=[done, *free], signal=act_done)
        sums_free = [out_]
        inv = dve.do(V.reciprocal, recip[:, par, :], buf[:, :, one], waits=[out_, *free], signal=dve_done)
        if unscale is not None:
            inv = dve.do(V.tensor_scalar, recip[:, par, :], recip[:, par, :], unscale, None, ALU.mult,
                         waits=[inv], signal=dve_done)
        a = out_
        for part in parts[1:]:
            a = pool.do(G.tensor_tensor, buf[:, :, 0:dh], buf[:, :, 0:dh], buf[:, :, part:part + dh], ALU.add,
                        waits=[a], signal=pool_done)
        a = pool.do(G.tensor_tensor, dst, buf[:, :, 0:dh],
                    recip[:, par, :].unsqueeze(2).broadcast_to([P, TB, dh]), ALU.mult,
                    waits=[a, inv, *dst_waits], signal=pool_done)
        o_sb.read_by(a)
        return a

    def interleave(main, side, start=0.04, end=1.0):
        whole, side_whole = sum(m[0] for m in main), sum(w for w, _ in side) or 1
        at, done, side_done = 0, 0, 0
        for work, step, _ in main:
            while at < len(side) and start + (end - start) * side_done / side_whole <= done / whole:
                side_done += side[at][0]
                at += 1
                side[at - 1][1]()
            step()
            done += work
        for _, step in side[at:]:
            step()

    def mingled(steps, others):
        every = len(steps) // (len(others) + 1)
        merged = []
        for n, step in enumerate(steps):
            merged.append(step)
            if n % every == every - 1 and n // every < len(others):
                merged.append(others[n // every])
        return merged

    def overlap_first(main, sides):
        for b, side in enumerate(sides):
            interleave([m for m in main if m[2] == b], side, start=0.0, end=0.9)

    projected = [(g, g.count) for g in (pe_rows, act_done, dve_done)]
    stack_free.append(projected)
    block_out = {}

    def self_sweep1(h, at_once=False):
        i = h % NSTACK

        def chunks(tile):
            n = (tile + 1) * P
            segments = [(k0, min(n, k0 + BQ), min(n, k0 + BQ) - k0) for k0 in range(0, n, BQ)]
            return [segments[c:c + 2] for c in range(0, len(segments), 2)]

        r = STACKED + 4
        return sweep1_steps(h, h, chunks, [(q_stack[i], k_stack[i])], mask_rows, lambda: [stack_ready[h]],
                            (q_stack[i][r:r + 1, :], q_stack[i][r + 1:r + 2, :]), maxrow_in[i],
                            1.0 / DH1 ** 0.5, at_once)

    def self_sweep2(h):
        i = h % NSTACK
        waiting = []
        steps = []

        def step(b, j):
            q0 = max(b * BQ, j * P)
            n = (b + 1) * BQ - q0
            slot, free = scores.take()
            diag = j >= TB * b
            scored = pe.do(TE.matmul, slot[:, 0:n], k_stack[i][:, j * P:(j + 1) * P], q_stack[i][:, q0:q0 + n],
                           start=True, stop=not diag, waits=[max_ready[h, b], *free], signal=pe_scores)
            if diag:
                scored = pe.do(TE.matmul, slot[:, 0:P], ident_bf[:, :], mask_cols[:, :], start=False,
                               stop=True, signal=pe_scores)
            s = step_count[0]
            step_count[0] += 1
            buf, hi, lo = weights(s, P, n, 1.0 / DH1 ** 0.5, scored)
            tiles = [(t, (TB * b + t) * P - q0) for t in range(TB) if TB * b + t >= j]
            waiting.append((b, j, buf, hi, lo, tiles))
            stack_last[i] = scored
            if len(waiting) > LAG:
                product()
            run_later()

        def product():
            b, j, buf, hi, lo, tiles = waiting.pop(0)
            done = attend(buf, hi, lo, P, tiles, j == 0, j == TB * b + TB - 1, v_self[:, j, h, :], 3 * DH1 + 1,
                          2 * DH1 + 1, TB, [v_ready, v_one])
            if j == TB * b + TB - 1:
                block_out[h, b] = finish_block(b % 2, done, TB, DH1, (0, DH1, 2 * DH1 + 1),
                                               o_self[:, TB * b:TB * b + TB, h * DH1:(h + 1) * DH1],
                                               [norm_t_read])
                if h == H - 1:
                    self_out(b)

        def drain():
            while waiting:
                product()
            stack_free[i] = [stack_last[i]]

        for b in range(NB):
            for j in range(TB * b + TB):
                steps.append((min(TB, TB * b + TB - j) + 1, lambda b=b, j=j: step(b, j), b))
        steps.append((1, drain, NB - 1))
        return steps

    stack_last = {}
    def project_out(src_t, weight, n, b, waits):
        slot, free = wide.take()
        for t in range(TB):
            for kc in range(n):
                done = pe.do(TE.matmul, slot[:, t * D:(t + 1) * D], src_t[:, kc, t * P:(t + 1) * P],
                             weight[:, kc, :], start=kc == 0, stop=kc == n - 1,
                             waits=[*waits, *free], signal=pe_rows)
        return slot[:, :].rearrange("p (t d) -> p t d", t=TB), done

    room = parts_room.empty()
    wq2, wk2 = ([room.take([DC, P], F32) for _ in range(2)] for _ in range(2))
    q_pair, k_pair = room.take([T], F32), room.take([SE], F32)
    wv2, wo2 = ([room.take([DC, D], F32) for _ in range(2)] for _ in range(2))
    bv2 = [room.take([D], F32) for _ in range(2)]
    HP = 2
    GH = D // DH2
    bq2, bk2 = room.take([H // HP], F32), room.take([H // HP], F32)
    v_pair = room.take([NS, HP * DH2], F32)
    v_top = room.take([2], F32)
    v_power = room.take([2], F32)
    v_scale, v_unscale = room.take([2], F32), room.take([2], F32)
    ctx_t = room.take([DC, SE], F32)
    o_cross = room.take([NT, D], F32)
    resid_room, *operand_rooms = [stack_rooms[h % NSTACK].empty() for h in range(H - NSTACK, H)]
    resid = resid_room.take([NT, D], F32)
    q_dup, q_low = zip(*[(r.take([T], F32R), r.take([T], F32R)) for r in operand_rooms])
    k_both, k_high = [], []
    VW2 = 2 * DH2 + 2
    v_cross = []
    ONE2 = DH2
    middle = nc.dram_tensor("x_middle", (T, D), F32, kind="Internal").ap()
    w_pair_ready, w_ready, cross_consts, cross_in = {}, {}, {}, {}
    resid_ready, norm_ready, normed = [], [], {}

    def load_group(g, waits):
        i, s = g % 2, w_cross_in[g % 2]
        cols = slice(g * D, (g + 1) * D)
        sp.do(SY.dma_start, wv2[i][:, :, :], A["wv2"][:, cols].rearrange("(c p) n -> p c n", p=P),
              waits=waits, signal=s, by=16)
        sp.do(SY.dma_start, bv2[i][:, :], A["bv2"][cols].partition_broadcast(P), waits=waits, signal=s, by=16)
        return sp.do(SY.dma_start, wo2[i][:, :, :], A["wo2"][cols, :].rearrange("(c p) n -> p c n", p=P),
                     waits=waits, signal=s, by=16)

    def load_pair(p, waits):
        for w, name in ((wq2, "wq2"), (wk2, "wk2")):
            done = sp.do(SY.dma_start, w[p % 2][:, :, :],
                         A[name][:, p * P:(p + 1) * P].rearrange("(c p) n -> p c n", p=P),
                         waits=waits, signal=w_pair_in[p % 2], by=16)
        return done

    def load_cross(waits):
        for p in range(2):
            w_pair_ready[p] = load_pair(p, waits)
        for dst, name in ((bq2, "bq2"), (bk2, "bk2")):
            cross_in["biases"] = sp.do(SY.dma_start, dst, A[name], waits=waits, signal=small_in, by=16)
        sp.do(SY.dma_start, o_cross[:, 0:NFULL, :],
              A["ctx"][0, 0:NFULL * P, :].rearrange("(t p) d -> p t d", p=P), signal=ctx_in, by=16)
        cross_in["ctx"] = sp.do(SY.dma_start, o_cross[0:S - NFULL * P, NFULL, :], A["ctx"][0, NFULL * P:S, :],
                                signal=ctx_in, by=16)
        for g in range(2):
            w_ready[g] = load_group(g, waits)

    def turn_context():
        def turn(b):
            rows = min(BQ, S - b * BQ)
            cross_in["ctx_t"] = transposed(o_cross[:, TB * b:, :], b, ctx_t, [cross_in["ctx"]], rows)
            cross_in["ctx_read"] = (pe_rows, pe_rows.count)
        return [(2, lambda b=b: turn(b)) for b in range(-(-S // BQ))]

    def self_out(b):
        x_slot, rows, loaded = load_block(A["x"][0], b)
        buf, free = o_t.take()

        def turn():
            moved = transposed(o_self[:, TB * b:TB * b + TB, :], 0, buf, [block_out[H - 1, b], *free])
            later.append([2, lambda: project(moved)])

        def project(moved):
            slot, done = project_out(buf, wo1, DC, b, [moved, w_self])
            o_t.read_by(done)
            added = dve.do(V.tensor_tensor, rows[:, :, :], slot, rows[:, :, :], ALU.add, waits=[done, loaded],
                           signal=dve_done)
            wide.read_by(added)
            cross_in["middle", b % 2] = sp.do(SY.dma_start, block_rows(middle, b), rows[:, :, :], waits=[added],
                                       signal=middle_out[b % 2], by=16)
            later.append([2, lambda: norm(added, cross_in["middle", b % 2])])

        def norm(added, stored_):
            ready = statistics(range(TB * b, TB * b + TB), rows, 0, [added])
            normed[b] = normalise(resid[:, TB * b:TB * b + TB, :], rows, b, [ready, *stack_free[(H - 3) % NSTACK]])
            x_blocks.read_by(normed[b], stored_, slot=x_slot)

        later.append([3, turn])

    kv_free = [(), ()]
    v_free = [(), ()]
    operands_ready, v_cross_ready = {}, {}

    pair_free, pair_ready = [()], {}

    def project_pair(p, queries=True, keys=True):
        tokens = []

        def project(w, bias, src, src_ready, dst, b, n):
            slot, free = wide.take()
            k0, k1 = 2 * b * BQ, min(n, 2 * (b + 1) * BQ)
            for b0 in range(k0, k1, BQ):
                b1 = min(k1, b0 + BQ)
                for kc in range(DC):
                    done = pe.do(TE.matmul, slot[:, b0 - k0:b1 - k0], w[p % 2][:, kc, :], src[:, kc, b0:b1],
                                 start=kc == 0, stop=kc == DC - 1,
                                 waits=[w_pair_ready[p], *src_ready, *free], signal=pe_rows)
            out_ = act.do(SC.activation, dst[:, k0:k1], slot[:, 0:k1 - k0], ACT.Identity, bias=bias[:, p:p + 1],
                          waits=[done, cross_in["biases"], *pair_free[0]], signal=act_done)
            wide.read_by(out_)
            tokens.append(out_)

        def end():
            pair_ready[p] = tokens[-1]
            if p + 2 < H // HP:
                w_pair_ready[p + 2] = load_pair(p + 2, [(pe_rows, pe_rows.count)])

        steps = []
        if keys:
            steps += [(7, lambda b=b: project(wk2, bk2, ctx_t, [cross_in["ctx_t"]], k_pair, b, S))
                      for b in range(2)]
        if queries:
            steps += [(7, lambda b=b: project(wq2, bq2, norm_t, norm_ready, q_pair, b, T)) for b in range(2)]
            steps.append((0, end))
        return steps

    def head_operands(h):
        i, r = h % 2, (h % HP) * DH2
        mine, low, high = slice(r, r + DH2), slice(0, DH2), slice(DH2, P)
        tokens = []

        def clear_rows():
            tokens.append(pool_alone(G.memset, q_low[i][DH2:DH2 + 2, :].bitcast(F32), 0.0,
                                     waits=[*kv_free[i]], signal=pool_done))

        def queries(b):
            c = slice(2 * b * BQ, 2 * (b + 1) * BQ)
            w = [pair_ready[h // HP], *kv_free[i]]
            hi_low = act.do(SC.copy, q_dup[i][low, c], q_pair[mine, c], waits=w, signal=act_done)
            hi_high = dve.do(V.tensor_copy, q_dup[i][high, c], q_pair[mine, c], waits=w, signal=dve_done)
            lo = dve.do(V.tensor_tensor, q_low[i][low, c], q_pair[mine, c], q_dup[i][mine, c].bitcast(F32),
                        ALU.subtract, waits=[hi_low, hi_high, cross_consts[i]], signal=dve_done)
            tokens.extend((hi_low, lo))

        def keys():
            c = slice(0, S)
            w = [pair_ready[h // HP], *kv_free[i]]
            hi = act.do(SC.copy, k_high[i][low, c], k_pair[mine, c], waits=[*w, cross_consts[i]], signal=act_done)
            own = dve.do(V.tensor_copy, k_both[i][mine, c], k_pair[mine, c], waits=[*w, cross_consts[i]],
                         signal=dve_done)
            lo = dve.do(V.tensor_tensor, k_both[i][high, c], k_pair[mine, c], k_both[i][mine, c].bitcast(F32),
                        ALU.subtract, waits=[own], signal=dve_done)
            tokens.extend((hi, lo))
            if r:
                tokens.append(act.do(SC.copy, k_both[i][low, c], k_pair[mine, c], signal=act_done))

        def ready():
            operands_ready[h] = [*tokens, cross_consts[i]]
            pair_free[0] = tuple(tokens)

        return [(0, clear_rows), (2, lambda: queries(0)), (2, lambda: queries(1)), (2, keys), (0, ready)]

    v_pair_free = [()]

    def head_values(pair):
        i, g = pair % 2, pair * HP // GH
        c0 = (pair * HP % GH) * DH2
        wd = HP * DH2
        tokens = []

        def tiles(t0):
            n = min(2 * TB, NS - t0)
            slot, free = wide.take()
            for t in range(t0, t0 + n):
                kw = min(P, S - t * P)
                for kc in range(DC):
                    done = pe.do(TE.matmul, slot[:kw, (t - t0) * wd:(t - t0 + 1) * wd],
                                 ctx_t[:, kc, t * P:t * P + kw], wv2[g % 2][:, kc, c0:c0 + wd],
                                 start=kc == 0, stop=kc == DC - 1,
                                 waits=[w_ready[g], cross_in["ctx_t"], *free], signal=pe_rows)
            for kw, ta, tb in ((P, t0, min(t0 + n, NFULL)), (S - NFULL * P, NFULL, t0 + n)):
                if ta < tb:
                    bias = bv2[g % 2][:kw, c0:c0 + wd].unsqueeze(1).broadcast_to([kw, tb - ta, wd])
                    src = slot[:kw, (ta - t0) * wd:(tb - t0) * wd].rearrange("p (t d) -> p t d", d=wd)
                    v = dve.do(V.tensor_tensor, v_pair[:kw, ta:tb, :], src, bias, ALU.add,
                               waits=[done, *v_pair_free[0], cross_consts["v_pair"]], signal=dve_done)
            wide.read_by(v)
            tokens.append(v)

        def split():
            top = dve.do(V.tensor_reduce, v_top[:, 0:1], v_pair[:, :, :], AX.XY, ALU.max,
                         apply_absolute_value=True, waits=[tokens[-1], *v_pair_free[0]], signal=dve_done)
            top = pool.do(G.partition_all_reduce, v_top[:, 1:2], v_top[:, 0:1], P, bass.bass_isa.ReduceOp.max,
                          waits=[top], signal=pool_done)
            pw, sc, un = (v[:, i:i + 1] for v in (v_power, v_scale, v_unscale))
            e = dve.do(V.tensor_scalar, pw, v_top[:, 1:2], 2.0 ** -100, None, ALU.max,
                       waits=[top, *v_free[i]], signal=dve_done)
            e = dve.do(V.tensor_scalar, pw.bitcast(mybir.dt.int32), pw.bitcast(mybir.dt.int32), 0x7F800000,
                       None, ALU.bitwise_and, waits=[e], signal=dve_done)
            e = dve.do(V.tensor_scalar, un, pw, 2.0 ** -V_BITS, None, ALU.mult,
                       waits=[e, *v_free[i]], signal=dve_done)
            e = dve.do(V.reciprocal, sc, un, waits=[e, *v_free[i]], signal=dve_done)
            full = v_pair[:, :, :].rearrange("p t (h d) -> p t h d", h=HP)
            for ta, tb in ((0, NS // 2), (NS // 2, NS)):
                hi = v_cross[i][:, ta:tb, :, 0:DH2]
                h_ = act.do(SC.activation, hi, full[:, ta:tb], ACT.Copy, scale=sc,
                            waits=[e, cross_consts[i], *v_free[i]], signal=act_done)
                v_cross_ready[pair] = dve.do(V.scalar_tensor_tensor,
                                             v_cross[i][:, ta:tb, :, ONE2 + 1:ONE2 + 1 + DH2],
                                             full[:, ta:tb], sc, hi, ALU.mult, ALU.subtract,
                                             waits=[h_, *v_free[i]], signal=dve_done)
            v_pair_free[0] = (v_cross_ready[pair],)

        return [(6, lambda t0=t0: tiles(t0)) for t0 in range(0, NS, 2 * TB)] + [(4, split)]

    CROSS_SCALE = 1.0 / DH2 ** 0.5

    def cross_sweep1(h, at_once=False):
        i = h % 2
        return sweep1_steps(h, H + h, lambda tile: CROSS_CHUNKS, [(q_dup[i], k_both[i]), (q_low[i], k_high[i])],
                            None, lambda: operands_ready[h],
                            (q_low[i][DH2:DH2 + 1, :], q_low[i][DH2 + 1:DH2 + 2, :]), maxrow_in[i], CROSS_SCALE,
                            at_once)

    QUARTER = (SE // 4) // 2 * 2
    LAST = S - 2 * QUARTER - (S - 2 * QUARTER) // 2
    LAST_AT = (S - LAST) // 2 * 2
    LAST = S - LAST_AT
    CROSS_CHUNKS = [[(0, QUARTER, QUARTER), (QUARTER, 2 * QUARTER, QUARTER)],
                    [(2 * QUARTER, 2 * QUARTER + LAST + LAST % 2, LAST),
                     (LAST_AT, LAST_AT + LAST + LAST % 2, LAST)]]

    def cross_sweep2(h):
        i, g = h % 2, h // GH
        pair = h // HP
        waiting, steps = [], []

        def step(b, j):
            kw = min(P, S - j * P)
            slot, free = scores.take()
            for n, (q, k) in enumerate([(q_dup[i], k_both[i]), (q_low[i], k_high[i])]):
                scored = pe.do(TE.matmul, slot[:kw, :], k[:, j * P:j * P + kw], q[:, b * BQ:(b + 1) * BQ],
                               start=n == 0, stop=n == 1, waits=[max_ready[H + h, b], *free], signal=pe_scores)
            s = step_count[0]
            step_count[0] += 1
            buf, hi, lo = weights(s, kw, BQ, CROSS_SCALE, scored)
            waiting.append((b, j, kw, buf, hi, lo))
            stack_last[i] = scored
            if len(waiting) > LAG:
                product()
            run_later()

        def product():
            b, j, kw, buf, hi, lo = waiting.pop(0)
            done = attend(buf, hi, lo, kw, [(t, t * P) for t in range(TB)], j == 0, j == NS - 1,
                          v_cross[pair % 2][:, j, h % HP, :], 2 * DH2 + 1, DH2 + 1, 2,
                          [v_cross_ready[pair]])
            if j == NS - 1:
                c0 = (h % GH) * DH2
                last = finish_block(b % 2, done, 2, DH2, (0, DH2 + 1),
                                    o_cross[:, TB * b:TB * b + TB, c0:c0 + DH2],
                                    [cross_in["ctx_read"], *o_read[b]], v_unscale[:, pair % 2:pair % 2 + 1])
                unscaled[pair % 2] = (dve_done, dve_done.count)
                if h % GH == GH - 1:
                    group_out(g, b, last)

        def drain():
            while waiting:
                product()
            kv_free[i] = [stack_last[i]]
            if h % HP == HP - 1:
                v_free[pair % 2] = [(pe_values, pe_values.count), unscaled[pair % 2]]

        for b in range(NB):
            for j in range(NS):
                steps.append((TB, lambda b=b, j=j: step(b, j), b))
        steps.append((1, drain, NB - 1))
        return steps

    o_read = [()] * NB
    unscaled = {}

    def group_out(g, b, last):
        buf, free = o_t.take()

        def turn():
            moved = transposed(o_cross[:, TB * b:TB * b + TB, :], 0, buf, [last, *free])
            o_read[b] = [(pe_rows, pe_rows.count)]
            later.append([2, lambda: project(moved)])

        def project(moved):
            slot, done = project_out(buf, wo2[g % 2], DC, b, [moved, w_ready[g]])
            o_t.read_by(done)
            rb = resid[:, TB * b:TB * b + TB, :]
            resid_ready[b] = dve.do(V.tensor_tensor, rb, slot, rb, ALU.add, waits=[done, resid_ready[b]],
                                    signal=dve_done)
            wide.read_by(resid_ready[b])
            if g == H // GH - 1:
                start_tail(b)
            if b == NB - 1 and g + 2 < H // GH:
                w_ready[g + 2] = load_group(g + 2, [(pe_rows, pe_rows.count)])

        later.append([3, turn])

    norm_room.empty()

    HT = TB // 2
    gamma, beta = norm_room.take([D], F32), norm_room.take([D], F32)
    bias8 = norm_room.take([D], BF16)
    w8_raw, w8 = norm_room.take([DC, D], BF16), norm_room.take([DC, D], BF16)
    x_bf, xq, y_bf = ([norm_room.take([HT, D], BF16) for _ in range(2)] for _ in range(3))
    xq_t = [norm_room.take([DC, HT * P], BF16) for _ in range(2)]
    scales, inv_scales = norm_room.take([2], F32), norm_room.take([2], F32)
    out_scale = norm_room.take([1], F32)
    row_top, row_spare, row_scale = ([norm_room.take([HT], F32) for _ in range(2)] for _ in range(3))
    row_scale_free = [(), ()]
    quant_y, quant_m = ([q_pair[:, i * HT * D:(i + 1) * HT * D] for i in n] for n in ((0, 1), (2, 3)))
    quant_free, x_bf_free, xq_free, xq_t_free, y_bf_free = ([(), ()] for _ in range(5))
    tail_state = {}

    def load_tail(waits):
        for dst, name in ((gamma, "gamma"), (beta, "beta"), (bias8, "bias8"), (scales[:, 0:1], "s_in"),
                          (scales[:, 1:2], "s_w")):
            sp.do(SY.dma_start, dst, A[name].partition_broadcast(P), waits=waits, signal=tails_in, by=16)
        tail_state["in"] = sp.do(SY.dma_start, w8_raw, A["w8"].rearrange("(c p) n -> p c n", p=P),
                                 waits=waits, signal=tails_in, by=16)

    def scale(i, src, inv_scale, waits):
        return act.do(SC.activation, quant_y[i], src, ACT.Copy, scale=inv_scale,
                      waits=[*waits, *quant_free[i]], signal=act_done)

    def quantise(i, scaled, dst, waits):
        y, m = quant_y[i], quant_m[i]
        e = dve.do(V.tensor_scalar, m.bitcast(mybir.dt.int32), y.bitcast(mybir.dt.int32), 0x7F800000, None,
                   ALU.bitwise_and, waits=[scaled, *quant_free[i]], signal=dve_done)
        e = dve.do(V.tensor_scalar, m, m, FP8_MIN_NORMAL, ROUND_TO_3_BITS, ALU.max, ALU.mult, waits=[e],
                   signal=dve_done)
        a = dve.do(V.tensor_tensor, y, y, m, ALU.add, waits=[e], signal=dve_done)
        a = dve.do(V.tensor_tensor, dst, y, m, ALU.subtract, waits=[a, *waits], signal=dve_done)
        quant_free[i] = (a,)
        return a

    def not_a_number_past_448(dst, src, spare, waits):
        e = dve.do(V.tensor_scalar, spare, src, FP8_MAX, -FP8_MAX, ALU.min, ALU.max, waits=waits,
                   signal=dve_done)
        e = dve.do(V.tensor_tensor, spare, src, spare, ALU.subtract, waits=[e], signal=dve_done)
        return dve.do(V.tensor_scalar, dst, spare, 3.0e38, 0.0, ALU.mult, ALU.mult, waits=[e], signal=dve_done)

    def tail_weights(waits):
        quant_free[0] = quant_free[1] = tuple(waits)
        inv = dve.do(V.reciprocal, inv_scales, scales, waits=[tail_state["in"]], signal=dve_done)
        tail_state["out_scale"] = dve.do(V.tensor_tensor, out_scale, scales[:, 0:1], scales[:, 1:2], ALU.mult,
                                         signal=dve_done)
        tail_state["inv"] = inv
        scaled = scale(0, w8_raw.rearrange("p c n -> p (c n)"), inv_scales[:, 1:2], [inv])
        flat = w8.rearrange("p c n -> p (c n)")
        rounded = quantise(0, scaled, flat, [])
        missing = not_a_number_past_448(quant_m[0], flat, quant_m[0], [rounded])
        tail_state["w8"] = dve.do(V.tensor_tensor, flat, flat, quant_m[0], ALU.add, waits=[missing],
                                  signal=dve_done)
        quant_free[0] = (tail_state["w8"],)

    def piece_stages(i, b, xb, loaded):
        half = slice(HT * i, HT * i + HT)
        tiles = range(TB * b + HT * i, TB * b + HT * i + HT)
        xr = xb[:, half, :]
        st = {}
        q, e, done_sig = (pool, G, pool_done) if b < NB - 1 else (dve, V, dve_done)

        def norm_statistics():
            st["beta"] = pool.do(G.tensor_tensor, xr, xr, beta.unsqueeze(1).broadcast_to([P, HT, D]), ALU.add,
                                 waits=[loaded, tail_state["in"]], signal=pool_done)
            st["stats"] = statistics(tiles, resid, TB * b + HT * i, [resid_ready[b]])

        def add_norm():
            for n, g in enumerate(tiles):
                row = resid[:, g, :]
                a = dve.do(V.scalar_tensor_tensor, row, row, meanvar[:, g, 0:1], gamma, ALU.subtract, ALU.mult,
                           waits=[st["stats"], tail_state["in"]], signal=dve_done)
                a = dve.do(V.scalar_tensor_tensor, xr[:, n, :], row, rstd[:, g:g + 1], xr[:, n, :], ALU.mult,
                           ALU.add, waits=[a, st["beta"]], signal=dve_done)
            st["stats"] = statistics(tiles, xr, 0, [a])

        def to_fp8():
            for n, g in enumerate(tiles):
                a = dve.do(V.tensor_scalar, x_bf[i][:, n, :], xr[:, n, :], meanvar[:, g, 0:1], rstd[:, g:g + 1],
                           ALU.subtract, ALU.mult, waits=[st["stats"], *x_bf_free[i]], signal=dve_done)
            st["scaled"] = scale(i, x_bf[i].rearrange("p t d -> p (t d)"), inv_scales[:, 0:1],
                                 [a, tail_state["inv"]])
            x_bf_free[i] = (st["scaled"],)

        def rounded():
            st["fp8"] = quantise(i, st["scaled"], xq[i].rearrange("p t d -> p (t d)"), xq_free[i])
            top = dve.do(V.tensor_reduce, row_top[i], xq[i], AX.X, ALU.max, apply_absolute_value=True,
                         waits=[st["fp8"]], signal=dve_done)
            missing = not_a_number_past_448(row_scale[i], row_top[i], row_spare[i],
                                            [top, *row_scale_free[i]])
            st["row_scale"] = dve.do(V.tensor_scalar, row_scale[i], row_scale[i], out_scale, None, ALU.add,
                                     waits=[missing, tail_state["out_scale"]], signal=dve_done)
            st["row_top"] = top

        def turn():
            slot, free = wide.take()
            half_t = slot[:, 0:BQ // 2].bitcast(BF16).rearrange("p (c t) -> p c t", c=DC)
            for n in range(HT):
                for c in range(DC):
                    tr = pe.do(TE.transpose, half_t[:, c, n * P:(n + 1) * P], xq[i][:, n, c * P:(c + 1) * P],
                               ident_bf[:, :], waits=[st["fp8"], *free], signal=pe_rows)
            xq_free[i] = (tr, st["row_top"])
            st["moved"] = act.do(SC.copy, xq_t[i], half_t, waits=[tr, *xq_t_free[i]], signal=act_done)
            wide.read_by(st["moved"])

        def product():
            slot, free = wide.take()
            for n in range(HT):
                for kc in range(DC):
                    done = pe.do(TE.matmul, slot[:, n * D:(n + 1) * D], xq_t[i][:, kc, n * P:(n + 1) * P],
                                 w8[:, kc, :], start=kc == 0, stop=kc == DC - 1,
                                 waits=[st["moved"], tail_state["w8"], *free], signal=pe_rows)
            xq_t_free[i] = (done,)
            for n in range(HT):
                y = act.do(SC.activation, y_bf[i][:, n, :], slot[:, n * D:(n + 1) * D], ACT.Copy,
                           scale=row_scale[i][:, n:n + 1], waits=[done, st["row_scale"], *y_bf_free[i]],
                           signal=act_done)
            row_scale_free[i] = (y,)
            wide.read_by(y)
            y = q.do(e.tensor_tensor, y_bf[i], y_bf[i], bias8.unsqueeze(1).broadcast_to([P, HT, D]), ALU.add,
                     waits=[y], signal=done_sig)
            st["y"] = y

        def store():
            added = q.do(e.tensor_tensor, xr, xr, y_bf[i], ALU.add, waits=[st["y"]], signal=done_sig)
            y_bf_free[i] = (added,)
            rows = out[0][b * BQ + i * HT * P:b * BQ + (i + 1) * HT * P, :].rearrange("(t p) d -> p t d", p=P)
            sp.do(SY.dma_start, rows, xr, waits=[added], signal=stored[b % 2], by=16)

        return [norm_statistics, add_norm, to_fp8, rounded, turn, product, store]

    def start_tail(b):
        slot, xb, loaded = load_block(middle, b, [cross_in["middle", 0], cross_in["middle", 1]])
        stages = [piece_stages(i, b, xb, loaded) for i in range(2)]
        for n in range(len(stages[0])):
            for i in range(2):
                later.append([TAIL_AT[n] + TAIL_APART * i, stages[i][n]])
        later.append([TAIL_AT[-1] + TAIL_APART,
                      lambda: x_blocks.read_by((stored[b % 2], stored[b % 2].count), slot=slot)])

    first = self_sweep1(0, at_once=True)
    for _, s in first[0]:
        s()
    first[1].append((0, lambda: load_stacks(1)))
    first[2].append((0, lambda: stack_free[2].append(fill_stack_constants(NSTACK - 1, projected))))
    first[3].append((0, lambda: load_stacks(2)))
    for h in range(H):
        if 0 < h < H - 2:
            load_stacks(h + 2)
        if h == H - NSTACK:
            load_cross([stack_ready[n] for n in range(H - NSTACK, H)])
        if h == 0:
            overlap_first(self_sweep2(0), first[1:] + [self_sweep1(1)])
        elif h < H - 1:
            context = turn_context() + project_pair(0, queries=False) if h == H - 2 else []
            interleave(self_sweep2(h), mingled(self_sweep1(h + 1), context), start=0.0, end=0.92)
        else:
            cross_consts["v_pair"] = pool.do(G.memset, v_pair[:, NS - 1, :], 0.0,
                                             waits=[stack_ready[n] for n in range(H - NSTACK, H)],
                                             signal=const_ready)
            *value_tiles, values_split = head_values(0)
            interleave(self_sweep2(h), value_tiles)

    while later:
        run_later()
    all_self = [(s, s.count) for s in (pe_rows, pe_scores, pe_values, act_done, exp_full, lo_dve, lo_pool,
                                       dve_max, dve_done, pool_done, *stack_in,
                                       *(s for row in maxrow_in for s in row))]
    s1.close()

    for i in range(2):
        k_both.append(sb(f"k_both{i}", [P, SE], F32R))
        k_high.append(sb(f"k_high{i}", [P, SE], F32R))
        v_cross.append(sb(f"v_cross{i}", [P, NS, HP, VW2], F16))
    bo2 = sb("bo2", [P, D], F32)
    bo2_loaded = sp.do(SY.dma_start, bo2[:, :], A["bo2"].partition_broadcast(P), waits=all_self,
                       signal=small_in, by=16)
    pool.do(None, waits=all_self)

    def fill_cross_constants(i):
        pool.do(G.memset, v_cross[i][:, :, :, ONE2:ONE2 + 1], 1.0, signal=const_ready)
        pool_alone(G.memset, q_low[i][DH2:P, :].bitcast(F32), 0.0, signal=const_ready)
        pool.do(G.memset, k_both[i][:, S:SE].bitcast(F32), 0.0, signal=const_ready)
        pool_alone(G.memset, k_high[i][0:DH2, S:SE].bitcast(F32), 0.0, signal=const_ready)
        z = pool_alone(G.memset, k_high[i][DH2:P, :].bitcast(F32), 0.0, signal=const_ready)
        cross_consts[i] = pool_alone(G.memset, k_high[i][DH2:DH2 + 2, :].bitcast(F32), 1.0, waits=[z],
                                     signal=const_ready)

    kv_free[:], v_free[:] = [all_self] * 2, [all_self] * 2
    fill_cross_constants(0)
    for b in range(NB):
        rb = resid[:, TB * b:TB * b + TB, :]
        norm_ready.append(transposed(rb, b, norm_t, [normed[b]]))
        resid_ready.append((act_done, act_done.count))
    fill_cross_constants(1)
    for b in range(NB):
        rb = resid[:, TB * b:TB * b + TB, :]
        resid_ready[b] = pool.do(G.tensor_tensor, rb, rb, bo2[:, :].unsqueeze(1).broadcast_to([P, TB, D]),
                                 ALU.add, waits=[norm_ready[b], bo2_loaded], signal=pool_done)

    first = cross_sweep1(0, at_once=True)
    for _, s in project_pair(0, keys=False) + head_operands(0) + first[0]:
        s()
    first[1].insert(0, values_split)
    for h in range(H):
        side = []
        if h == H - HP:
            load_tail([(pe_rows, pe_rows.count)])
        if h == H - 1:
            tail_weights(pair_free[0])
        if h + 1 < H:
            if (h + 1) % HP == 0:
                side += project_pair((h + 1) // HP)
            side += head_operands(h + 1)
            if (h + 1) % HP == 0:
                side += head_values((h + 1) // HP)
            else:
                side.append((OPERANDS_LAG, lambda: None))
            side += cross_sweep1(h + 1)
        if h == 0:
            overlap_first(cross_sweep2(0), first[1:] + [side])
        else:
            interleave(cross_sweep2(h), side)
    while later:
        run_later()


    sp.do(None, waits=[(sem_, sem_.count) for sem_ in stored])

    block = ctx.enter_context(nc.Block())

    @block.tensor
    def _(e):
        pe.run(e)

    @block.scalar
    def _(e):
        act.run(e)

    @block.vector
    def _(e):
        dve.run(e)

    @block.gpsimd
    def _(e):
        pool.run(e)

    @block.sync
    def _(e):
        sp.run(e)


def kernel(x, ctx_1024, L0_attn_Wq, L0_attn_Wk, L0_attn_Wv, L0_attn_Wo, L0_xattn_Wq, L0_xattn_bq,
           L0_xattn_Wk, L0_xattn_bk, L0_xattn_Wv, L0_xattn_bv, L0_xattn_Wo, L0_xattn_bo,
           L0_xattn_ln_gamma, L0_xattn_ln_beta, L0_ffn_kernel, L0_ffn_input_scale,
           L0_ffn_kernel_scale, L0_ffn_bias):
    import concourse.bacc as bacc
    from concourse.bass_utils import run_bass_kernel_spmd

    arrays = {
        "x": x, "ctx": ctx_1024,
        "wq1": np.asarray(L0_attn_Wq).T, "wk1": np.asarray(L0_attn_Wk).T,
        "wv1": np.asarray(L0_attn_Wv).T, "wo1": np.asarray(L0_attn_Wo).T,
        "wq2": L0_xattn_Wq, "wk2": L0_xattn_Wk,
        "wv2": L0_xattn_Wv, "bv2": L0_xattn_bv, "wo2": L0_xattn_Wo, "bo2": L0_xattn_bo,
        "bq2": np.asarray(L0_xattn_bq).reshape(-1, P).T, "bk2": np.asarray(L0_xattn_bk).reshape(-1, P).T,
        "gamma": L0_xattn_ln_gamma, "beta": L0_xattn_ln_beta,
        "w8": L0_ffn_kernel, "s_in": L0_ffn_input_scale, "s_w": L0_ffn_kernel_scale,
        "bias8": L0_ffn_bias, "alibi": alibi_rows(),
    }
    arrays = {f"{n}_dram": np.ascontiguousarray(a) for n, a in arrays.items()}
    nc = bacc.Bacc("TRN2", target_bir_lowering=False, num_devices=1)
    ins = {n[:-5]: nc.dram_tensor(n, a.shape, mybir.dt.from_np(a.dtype), kind="ExternalInput").ap()
           for n, a in arrays.items()}
    out = nc.dram_tensor("out_dram", (1, T, D), F32, kind="ExternalOutput").ap()
    decoder(nc, ins, out)
    return run_bass_kernel_spmd(nc, [arrays], core_ids=[0]).results[0]["out_dram"]
```
